# Optimizing a Trainium2 kernel written in Bass

```python
import numpy as np
import jax
import jax.numpy as jnp

def _softmax(x, axis=-1):
    return jax.nn.softmax(x, axis=axis)

def _gelu(x):
    return jax.nn.gelu(x, approximate=True)

def _silu(x):
    return jax.nn.silu(x)

def _sigmoid(x):
    return jax.nn.sigmoid(x)

def _layernorm(x, axis=-1, eps=1e-05):
    m = jnp.mean(x, axis=axis, keepdims=True)
    v = jnp.var(x, axis=axis, keepdims=True)
    return (x - m) / jnp.sqrt(v + eps)

def _scatter_add(tgt, idx, src, axis=0):
    return tgt.at[idx].add(src)

def _segment_sum(src, seg, n):
    return jax.ops.segment_sum(src, seg, n)
kernel_name = 'mk_gnn_resnorm_d1_gnn_r64_1f30db'

def setup_inputs(seed: int=0):
    np.random.seed(seed)
    _w = jnp.asarray

    def _rec_inputs():
        import jax
        import jax.numpy as jnp
        _gk = jax.random.key(seed)
        x = -0.0002117 + 1 * jax.random.normal(jax.random.fold_in(_gk, 1), (100000, 256), jnp.float32)
        src = jax.random.randint(jax.random.fold_in(_gk, 2), (25000,), 0, 100000, jnp.int32)
        dst = jnp.minimum((100000 * jax.random.uniform(jax.random.fold_in(_gk, 3), (25000,)) ** 2.0).astype(jnp.int32), 99999)
        _o = jnp.argsort(dst, stable=True)
        src = src[_o]
        dst = dst[_o]
        edge_weight = 3.40706e-05 + 0.0312496 * jax.random.normal(jax.random.fold_in(_gk, 12), (25000,), jnp.float32)
        return (x, src, dst, edge_weight)
    x, src, dst, edge_weight = _rec_inputs()

    def _L0_gnn_setup():
        import jax, jax.numpy as jnp
        import numpy as np
        N = 100000
        E = 50000
        C_IN = 256
        C_OUT = 256
        CONV_ORDER = 3
        key = jax.random.key(seed)
        k1, k2, k3, k4, k5 = jax.random.split(key, 5)
        x = jax.random.normal(k1, (N, C_IN), dtype=jnp.float32)
        edge_row = jax.random.randint(k2, (E,), 0, N, dtype=jnp.int32)
        edge_col = jax.random.randint(k3, (E,), 0, N, dtype=jnp.int32)
        edge_val = jax.random.normal(k4, (E,), dtype=jnp.float32) * (1.0 / 32.0)
        fan_in, fan_out = (C_IN, C_OUT)
        bound = 1.414 * np.sqrt(6.0 / (fan_in + fan_out))
        weight = jax.random.uniform(k5, (C_IN, C_OUT, 1 + CONV_ORDER), dtype=jnp.float32, minval=-bound, maxval=bound)
        return {'x': x, 'edge_row': edge_row, 'edge_col': edge_col, 'edge_val': edge_val, 'weight': weight}
    _L0_gnn_all = _L0_gnn_setup()
    _L0_gnn_in = {k: v for k, v in _L0_gnn_all.items() if k in ('weight',)}
    del _L0_gnn_all
    return {'x': x, 'src': src, 'dst': dst, 'edge_weight': edge_weight, 'L0_gnn_weight': _L0_gnn_in['weight']}

def reference(x, src, dst, edge_weight, L0_gnn_weight):
    import jax
    import jax.numpy as jnp

    def _L0_gnn_ref(x, edge_row, edge_col, edge_val, weight):
        import jax, jax.numpy as jnp
        import numpy as np
        N = 100000
        E = 50000
        C_IN = 256
        C_OUT = 256
        CONV_ORDER = 3
        'GCNLayer.forward: Chebyshev hops of sparse Laplacian + weighted combine.\n\n            x: [N, C_in]; laplacian in COO (edge_row, edge_col, edge_val); weight: [C_in, C_out, 1+K].\n            Returns [N, C_out].\n            '
        n = x.shape[0]

        def spmm(v):
            return jax.ops.segment_sum(edge_val[:, None] * v[edge_col], edge_row, num_segments=n)
        hops = []
        h = x
        for _ in range(CONV_ORDER):
            h = spmm(h)
            hops.append(h)
        X = jnp.stack([x] + hops, axis=2)
        return jnp.einsum('nik,iok->no', X, weight)
    x = _layernorm(x + _L0_gnn_ref(x, src, dst, edge_weight, L0_gnn_weight), axis=-1)
    return x

_drawn_inputs = setup_inputs


def setup_inputs(seed=0):
    import zlib

    import numpy as np

    out = dict(_drawn_inputs(seed))
    spreads = {}
    factors = {'edge_weight': 4.415}
    for name, (base, spread) in spreads.items():
        noise = np.random.default_rng([zlib.crc32(name.encode()), seed]).standard_normal(out[name].shape)
        drawn = base * np.exp(spread * noise) if base else spread * noise
        out[name] = jnp.asarray(drawn.astype(out[name].dtype))
    for name, factor in factors.items():
        out[name] = (out[name] * factor).astype(out[name].dtype)
    return out
```

```python
from contextlib import ExitStack

import concourse.bass as bass
from concourse import mybir

P = 128
F32 = mybir.dt.float32
F16 = mybir.dt.float16
BF16 = mybir.dt.bfloat16
I32 = mybir.dt.int32
ALU = mybir.AluOpType
ACT = mybir.ActivationFunctionType

EPS = 1e-5
UNROLL = 4
NOWHERE = 1 << 20


def at_least(eng, sem, value):
    if isinstance(value, int) and value <= 0:
        return
    eng.wait_ge(sem, value)


def gnn_program(nc, x, row, col, value, weight, out):
    N, C = x.shape
    E = row.shape[0]
    CO = weight.shape[1]
    HOPS = weight.shape[2] - 1
    KC = C // P
    TILES = -(-E // (P * UNROLL)) * UNROLL
    E_PAD = TILES * P
    STEPS = 2 * TILES
    ITS = STEPS // UNROLL
    PH = TILES // UNROLL
    ROWS = 2 * P
    DENSE = N // ROWS
    TAIL = N - DENSE * ROWS
    TAIL_P = TAIL // 2
    META = TILES + UNROLL
    NT = -(-N // P)
    EROWS = TILES // 2
    LO = 256
    HI = N // LO + 2
    PAD_ROW = (HI - 1) * LO
    REC = 4
    DITS = 2 * ITS
    assert C == 2 * P and CO == 2 * P and HOPS == 3 and TILES % UNROLL == 0
    assert 2 * (DITS - 1) <= DENSE < 2 * DITS - 1 and TAIL % 2 == 0 and 0 < TAIL_P <= P
    assert N <= PAD_ROW < NOWHERE and LO <= 512 and HI <= 512

    h1_rows = nc.dram_tensor("h1_rows", (E_PAD, C), F32, kind="Internal").ap()
    h2_rows = nc.dram_tensor("h2_rows", (E_PAD, C), F32, kind="Internal").ap()
    place_of = nc.dram_tensor("place_of", (NT * P, 1), I32, kind="Internal").ap()
    by_lo = nc.dram_tensor("by_lo", (E_PAD, REC), I32, kind="Internal").ap()
    by_row = nc.dram_tensor("by_row", (E_PAD, REC), I32, kind="Internal").ap()
    row_line = nc.dram_tensor("row_line", (1 + 2 * E_PAD,), F32, kind="Internal").ap()

    with ExitStack() as ctx:
        def sb(name, shape, dt=F32):
            return ctx.enter_context(nc.sbuf_tensor(name, shape, dt))

        def sem(name):
            return ctx.enter_context(nc.semaphore(name))

        def sems(name, n=UNROLL):
            return [sem(f"{name}{i}") for i in range(n)]

        ident = sb("ident", [P, P])
        w_raw = sb("w_raw", [P, KC, CO * (HOPS + 1)])
        w_sb = sb("w_sb", [P, HOPS + 1, KC, CO])
        eps = sb("eps", [P, 1])
        ident_b = sb("ident_b", [P, P], BF16)
        ones = sb("ones", [P, P])
        below = sb("below", [P, P])
        counter_i = sb("counter_i", [P, HI], I32)
        counter = sb("counter", [P, HI])
        counter_h = sb("counter_h", [P, HI], F16)
        row_in = sb("row_in", [P, TILES], I32)
        col_in = sb("col_in", [P, TILES], I32)
        val_in = sb("val_in", [P, TILES])
        rec = sb("rec", [P, TILES, REC], I32)
        digit_i = sb("digit_i", [P, TILES], I32)
        digit = sb("digit", [P, TILES])
        hot = sb("hot", [P, UNROLL, HI], BF16)
        counts = sb("counts", [P, HI])
        upto = sb("upto", [P, HI])
        ones_w = sb("ones_w", [P, HI])
        place = sb("place", [P, HI])
        picked = sb("picked", [P, HI])
        place_f = sb("place_f", [P, UNROLL])
        rec_idx = sb("rec_idx", [P, UNROLL], I32)
        rec_out = sb("rec_out", [P, UNROLL, REC], I32)
        rec_r = sb("rec_r", [EROWS, 2 * P, REC], I32)
        next_r = sb("next_r", [EROWS, 2 * P, REC], I32)
        val_r = sb("val_r", [EROWS, 2 * P])
        col_r = sb("col_r", [EROWS, 2 * P])
        row_r = sb("row_r", [EROWS, 2 * P])
        last_r = sb("last_r", [EROWS, 2 * P])
        tidx_r = sb("tidx_r", [EROWS, 2 * P])
        before = sb("before", [1, 1])
        nowhere = sb("nowhere", [P, NT], I32)
        meta = sb("meta", [P, META, 4], I32)
        d_col = sb("d_col", [P, STEPS])
        w_col = sb("w_col", [P, STEPS])
        a_idx = sb("a_idx", [P, UNROLL, 3], I32)
        q_src = sb("q_src", [P, UNROLL], I32)
        q_got = sb("q_got", [P, UNROLL], I32)
        h_idx = sb("h_idx", [P, UNROLL], I32)
        c_idx = sb("c_idx", [P, UNROLL, 3], I32)
        o_idx = sb("o_idx", [P, UNROLL], I32)
        dst_b = sb("dst_b", [P, 2, 2 * P + 1])
        gath = sb("gath", [P, UNROLL, C])
        S = sb("S", [P, UNROLL, P])
        same = sb("same", [P, UNROLL, P])
        hT = sb("hT", [P, UNROLL, KC, P])
        h_row = sb("h_row", [P, UNROLL, C])
        x_in = sb("x_in", [P, 2, 2, C])
        xT = sb("xT", [P, 2, 2, KC, P])
        stats = sb("stats", [P, 2, 2, 6])
        mv = sb("mv", [P, 2, 2, 2])
        std = sb("std", [P, 2, 2])
        rstd = sb("rstd", [P, 2, 2])
        nmr = sb("nmr", [P, 2, 1])
        y_out = sb("y_out", [P, 2, 2, CO])
        x_dst = sb("x_dst", [P, UNROLL, C])
        h_in = sb("h_in", [P, UNROLL, 2, C])
        cT = sb("cT", [P, UNROLL, 6, P])
        res = sb("res", [P, UNROLL, CO])

        ps_x = [ctx.enter_context(nc.psum_tensor(f"ps_x{i}", [P, 4, P], F32)) for i in range(2)]
        ps_y = [ctx.enter_context(nc.psum_tensor(f"ps_y{i}", [P, 2, CO], F32)) for i in range(2)]
        ps_h = [ctx.enter_context(nc.psum_tensor(f"ps_h{i}", [P, 4, P], F32)) for i in range(2)]
        ps_r = [ctx.enter_context(nc.psum_tensor(f"ps_r{i}", [P, 4, P], F32)) for i in range(2)]

        pads_set = sem("pads_set")
        edges_in = sem("edges_in")
        w_in = sem("w_in")
        consts_set = sem("consts_set")
        counter_set = sem("counter_set")
        digits_set = sem("digits_set")
        hot_built = sem("hot_built")
        hot_used = sem("hot_used")
        counted = sem("counted")
        counts_read = sem("counts_read")
        based = sem("based")
        upto_set = sem("upto_set")
        place_set = sem("place_set")
        place_moved = sem("place_moved")
        rec_staged = sem("rec_staged")
        rec_landed = sems("rec_landed")
        by_lo_in = sem("by_lo_in")
        by_row_in = sem("by_row_in")
        cols_f = sem("cols_f")
        line_out = sem("line_out")
        table_out = sem("table_out")
        last_set = sem("last_set")
        shifted = sem("shifted")
        meta_turned = sem("meta_turned")
        meta_cleared = sem("meta_cleared")
        places_set = sem("places_set")
        w_split = sem("w_split")
        setup_done = sem("setup_done")
        meta_ready = sem("meta_ready")
        pool_goes = sem("pool_goes")
        x_landed = sems("x_landed", 2)
        dst_landed = sems("dst_landed", 2)
        g_landed = sems("g_landed")
        t_landed = sems("t_landed")
        q_landed = sems("q_landed")
        h_stored = sems("h_stored")
        y_stored = sems("y_stored", 2)
        staged = sem("staged")
        q_used = sem("q_used")
        s_built = sem("s_built")
        x_turned = sem("x_turned")
        xT_ready = sem("xT_ready")
        y_summed = sem("y_summed")
        h_summed = sem("h_summed")
        hT_ready = sem("hT_ready")
        h_turned = sem("h_turned")
        h_row_ready = sem("h_row_ready")
        stats_ready = sem("stats_ready")
        mv_ready = sem("mv_ready")
        std_ready = sem("std_ready")
        rstd_ready = sem("rstd_ready")
        y0_ready = sem("y0_ready")
        y1_ready = sem("y1_ready")
        c_dst_landed = sems("c_dst_landed", 2)
        c_h_landed = sems("c_h_landed")
        c_x_landed = sems("c_x_landed")
        c_g_landed = sems("c_g_landed")
        c_stored = sems("c_stored")
        c_staged = sem("c_staged")
        c_out_staged = sem("c_out_staged")
        c_s_built = sem("c_s_built")
        c_turned = sem("c_turned")
        c_T_ready = sem("c_T_ready")
        c_h_summed = sem("c_h_summed")
        c_hT_ready = sem("c_hT_ready")
        c_y_summed = sem("c_y_summed")
        c_stats_ready = sem("c_stats_ready")
        c_mv_ready = sem("c_mv_ready")
        c_std_ready = sem("c_std_ready")
        c_rstd_ready = sem("c_rstd_ready")
        c_ready = sem("c_ready")

        def uses(it, j, d=0):
            return it + (j + d) // UNROLL + 1

        def dense_nodes(d):
            return P if not isinstance(d, int) or d < DENSE else TAIL_P if d == DENSE else 0

        def x_or_out(a, t):
            return a[bass.ds(t * ROWS, ROWS), :].rearrange("(p r) c -> p r c", r=2)

        def tail_of(a):
            return a[DENSE * ROWS:N, :].rearrange("(p r) c -> p r c", r=2)

        def dst_pair(h):
            return row_line[bass.ds(h * 2 * P, 2 * P + 1)].rearrange(
                "(o n) -> o n", o=1).broadcast_to((P, 2 * P + 1))

        block = ctx.enter_context(nc.Block())

        @block.sync
        def _(sp):
            sp.wait_ge(pads_set, 1)
            full = E // TILES
            for tile, a in ((row_in, row), (col_in, col), (val_in, value)):
                sp.dma_start(tile[0:full, :], a[0:full * TILES].rearrange("(p t) -> p t", t=TILES)
                             ).then_inc(edges_in, 16)
                sp.dma_start(tile[full:full + 1, 0:E - full * TILES],
                             a[full * TILES:E].rearrange("(o n) -> o n", o=1)).then_inc(edges_in, 16)
            sp.dma_start(w_raw[:], weight.rearrange("(k p) o h -> p k (o h)", p=P)).then_inc(w_in, 16)
            sp.dma_start(x_in[:, 0], x_or_out(x, 0)).then_inc(x_landed[0], 16)
            sp.dma_start(place_of.rearrange("(p t) o -> p (t o)", p=P), nowhere[:]).then_inc(table_out, 16)

            def dense(dit, jd):
                d = dit * 2 + jd
                fixed = isinstance(d, int)
                slot = (jd + 1) % 2
                if not fixed or d + 1 <= DENSE:
                    at_least(sp, x_turned, d)
                    if fixed and d + 1 == DENSE:
                        sp.dma_start(x_in[0:TAIL_P, slot], tail_of(x)).then_inc(x_landed[slot], 16)
                    else:
                        sp.dma_start(x_in[:, slot], x_or_out(x, d + 1)).then_inc(x_landed[slot], 16)
                if not fixed or d > 0:
                    sp.wait_ge(y1_ready, d)
                    if fixed and d - 1 == DENSE:
                        sp.dma_start(tail_of(out), y_out[0:TAIL_P, slot]).then_inc(y_stored[slot], 16)
                    else:
                        sp.dma_start(x_or_out(out, d - 1), y_out[:, slot]).then_inc(y_stored[slot], 16)

            dense(0, 0)
            dense(0, 1)
            with sp.Fori(1, PH) as it:
                dense(it, 0)
                dense(it, 1)
            for j in range(UNROLL):
                sp.wait_ge(rec_landed[j], 16 * PH)
            sp.dma_start(rec[:], by_lo.rearrange("(p t) w -> p t w", t=TILES)).then_inc(by_lo_in, 16)
            with sp.Fori(PH, ITS) as it:
                dense(it, 0)
                dense(it, 1)
            for j in range(UNROLL):
                sp.wait_ge(rec_landed[j], 16 * ITS)
            sp.dma_start(rec_r[:], by_row.rearrange("(r n) w -> r n w", n=2 * P)).then_inc(by_row_in, 16)
            sp.dma_start(next_r[0:EROWS - 1], by_row[1:1 + (EROWS - 1) * 2 * P, :].rearrange(
                "(r n) w -> r n w", n=2 * P)).then_inc(by_row_in, 16)
            sp.dma_start(next_r[EROWS - 1:EROWS, 0:2 * P - 1], by_row[1 + (EROWS - 1) * 2 * P:E_PAD, :].rearrange(
                "(o n) w -> o n w", o=1)).then_inc(by_row_in, 16)
            sp.wait_ge(cols_f, 1)
            sp.dma_start(row_line[0:1].rearrange("(o n) -> o n", o=1), before[:]).then_inc(line_out, 16)
            for k in range(2):
                sp.dma_start(row_line[1 + k * E_PAD:1 + (k + 1) * E_PAD].rearrange("(r n) -> r n", n=2 * P),
                             row_r[:]).then_inc(line_out, 16)
            sp.wait_ge(line_out, 48)
            sp.dma_start(dst_b[:, 0], dst_pair(0)).then_inc(dst_landed[0], 16)

            def step(it, j, more_dst, h_rows):
                t = it * UNROLL + j
                if j % 2 == 0:
                    dense(it + ITS, j // 2)
                if j % 2 == 0 and more_dst:
                    at_least(sp, s_built, t)
                    half = (j // 2 + 1) % 2
                    sp.dma_start(dst_b[:, half], dst_pair(it * 2 + j // 2 + 1)).then_inc(dst_landed[half], 16)
                slot = (j - 1) % UNROLL
                if h_rows is not None:
                    sp.wait_ge(h_row_ready, t)
                    first = 0 if h_rows is h1_rows else TILES
                    sp.dma_start(h_rows[bass.ds((t - 1 - first) * P, P), :], h_row[:, slot]
                                 ).then_inc(h_stored[slot], 16)

            for j in range(UNROLL):
                step(0, j, True, h1_rows if j else None)
            with sp.Fori(1, PH) as it:
                for j in range(UNROLL):
                    step(it, j, True, h1_rows)
            for j in range(UNROLL):
                step(PH, j, True, h2_rows if j else h1_rows)
            with sp.Fori(PH + 1, ITS - 2) as it:
                for j in range(UNROLL):
                    step(it, j, True, h2_rows)
            for it in (ITS - 2, ITS - 1):
                for j in range(UNROLL):
                    step(it, j, it * UNROLL + j + 2 < STEPS, h2_rows)
            sp.wait_ge(h_row_ready, STEPS)
            sp.dma_start(h2_rows[E_PAD - P:E_PAD, :], h_row[:, UNROLL - 1]).then_inc(h_stored[UNROLL - 1], 16)

            for j in range(UNROLL):
                sp.wait_ge(h_stored[j], 16 * ITS)
            sp.wait_ge(s_built, STEPS)

            def load_h(i, slot):
                for k, rows in enumerate((h1_rows, h2_rows)):
                    sp.dma_start(h_in[:, slot, k], rows[bass.ds(i * P, P), :]).then_inc(c_h_landed[slot], 16)

            sp.dma_start(dst_b[:, 0], dst_pair(0)).then_inc(c_dst_landed[0], 16)
            for i in range(UNROLL - 1):
                load_h(i, i)

            def finish(it, j):
                i = it * UNROLL + j
                last = isinstance(it, int) and it == PH - 1
                if not last or j == 0:
                    at_least(sp, c_turned, i)
                    load_h(i + UNROLL - 1, (j + UNROLL - 1) % UNROLL)
                if j % 2 == 0 and not (last and j == 2):
                    at_least(sp, c_s_built, i)
                    half = (j // 2 + 1) % 2
                    sp.dma_start(dst_b[:, half], dst_pair(it * 2 + j // 2 + 1)).then_inc(c_dst_landed[half], 16)

            for j in range(UNROLL):
                finish(0, j)
            with sp.Fori(1, PH - 1) as it:
                for j in range(UNROLL):
                    finish(it, j)
            for j in range(UNROLL):
                finish(PH - 1, j)
            for j in range(UNROLL):
                sp.wait_ge(c_stored[j], 16 * PH)

        @block.gpsimd
        def _(pool):
            nc.gpsimd.memset(ident[:], 0.0)
            nc.gpsimd.memset(ones[:], 1.0).then_inc(consts_set, 1)
            nc.gpsimd.iota(counter_i[:], pattern=[[1, HI]], base=0, channel_multiplier=0).then_inc(counter_set, 1)
            pool.wait_ge(consts_set, 1)
            nc.gpsimd.affine_select(out=ident[:], in_=ident[:], compare_op=ALU.not_equal, fill=1.0,
                                    base=0, pattern=[[-1, P]], channel_multiplier=1).then_inc(consts_set, 1)
            nc.gpsimd.affine_select(out=below[:], in_=ones[:], compare_op=ALU.is_gt, fill=0.0,
                                    base=0, pattern=[[1, P]], channel_multiplier=-1).then_inc(consts_set, 1)
            pool.wait_ge(meta_cleared, 1)
            nc.gpsimd.iota(meta[:, 0:TILES, 2], pattern=[[P, TILES]], base=0,
                           channel_multiplier=1).then_inc(places_set, 1)
            limit_nodes, limit_places = (pool.to_reg(n - 1) for n in (N, E_PAD))

            def go():
                pool.sem_inc(pool_goes, 1)

            def gather(dst_ap, rows, idx, limit, landed):
                nc.gpsimd.indirect_dma_start(
                    dst_ap, None, rows[:, :], bass.IndirectOffsetOnAxis(ap=idx, axis=0),
                    bounds_check=limit, oob_is_err=False).then_inc(landed, 16)

            def scatter(rows, idx, limit, src_ap, landed):
                nc.gpsimd.indirect_dma_start(
                    rows[:, :], bass.IndirectOffsetOnAxis(ap=idx, axis=0), src_ap, None,
                    bounds_check=limit, oob_is_err=False).then_inc(landed, 16)

            def sort(it, j, rows):
                pool.wait_ge(rec_staged, it * UNROLL + j + 1)
                go()
                scatter(rows, rec_idx[:, j:j + 1], limit_places, rec_out[:, j], rec_landed[j])

            for first, rows in ((0, by_lo), (PH, by_row)):
                with pool.Fori(first, first + PH) as it:
                    for j in range(UNROLL):
                        sort(it, j, rows)

            pool.wait_ge(table_out, 16)

            def hop1(it, j):
                t = it * UNROLL + j
                at_least(pool, h_summed, t - UNROLL + 1)
                pool.wait_ge(staged, t + 1)
                go()
                gather(gath[:, j], x, a_idx[:, j, 0:1], limit_nodes, g_landed[j])
                scatter(place_of, a_idx[:, j, 1:2], limit_nodes, a_idx[:, j, 2:3], t_landed[j])

            for j in range(UNROLL):
                hop1(0, j)
            with pool.Fori(1, PH) as it:
                for j in range(UNROLL):
                    hop1(it, j)

            for j in range(UNROLL):
                pool.wait_ge(t_landed[j], 16 * PH)

            def ask(j):
                gather(q_got[:, j:j + 1], place_of, q_src[:, j:j + 1], limit_nodes, q_landed[j])

            pool.wait_ge(q_used, UNROLL)
            for j in range(UNROLL):
                ask(j)
            for j in range(UNROLL):
                pool.wait_ge(h_stored[j], 16 * PH)

            def hop2(it, j, more):
                t = it * UNROLL + j
                pool.wait_ge(q_used, t - TILES + UNROLL + 1)
                pool.wait_ge(h_summed, t - UNROLL + 1)
                go()
                if more:
                    ask(j)
                gather(gath[:, j], h1_rows, h_idx[:, j:j + 1], limit_places, g_landed[j])

            with pool.Fori(PH, ITS - 1) as it:
                for j in range(UNROLL):
                    hop2(it, j, True)
            for j in range(UNROLL):
                hop2(ITS - 1, j, False)

            for j in range(UNROLL):
                pool.wait_ge(h_stored[j], 16 * ITS)
            for j in range(2):
                pool.wait_ge(y_stored[j], 16 * ((DENSE - j) // 2 + 1))
            pool.wait_ge(h_summed, STEPS)

            def finish(it, j, behind=True, now=True):
                i = it * UNROLL + j
                if now:
                    at_least(pool, c_turned, i - UNROLL + 1)
                    at_least(pool, c_h_summed, i - UNROLL + 1)
                    pool.wait_ge(c_staged, i + 1)
                    go()
                    gather(x_dst[:, j], x, c_idx[:, j, 0:1], limit_nodes, c_x_landed[j])
                    gather(gath[:, j], h2_rows, c_idx[:, j, 2:3], limit_places, c_g_landed[j])
                if behind:
                    slot = (j - 3) % UNROLL
                    pool.wait_ge(c_out_staged, i - 2)
                    pool.wait_ge(c_ready, i - 2)
                    go()
                    scatter(out, o_idx[:, slot:slot + 1], limit_nodes, res[:, slot], c_stored[slot])

            for j in range(UNROLL):
                finish(0, j, behind=j >= 3)
            with pool.Fori(1, PH) as it:
                for j in range(UNROLL):
                    finish(it, j)
            for j in range(3):
                finish(PH, j, now=False)

        @block.tensor
        def _(pe):
            pe.wait_ge(setup_done, 1)
            pe.wait_ge(consts_set, 3)

            def turn_x(dit, jd, n=P):
                d = dit * 2 + jd
                pe.wait_ge(x_landed[jd], 16 * (dit + 1))
                at_least(pe, xT_ready, d - 1)
                for r in range(2):
                    for k in range(KC):
                        last = nc.tensor.transpose(ps_x[jd][:, 2 * r + k, 0:n],
                                                   x_in[0:n, jd, r, k * P:(k + 1) * P], ident[0:n, 0:n])
                last.then_inc(x_turned, 1)

            def sum_y(dit, jd, n=P):
                d = dit * 2 + jd
                pe.wait_ge(xT_ready, d + 1)
                at_least(pe, y1_ready, d - 1)
                for r in range(2):
                    for k in range(KC):
                        last = nc.tensor.matmul(ps_y[jd][0:n, r], xT[:, jd, r, k, 0:n],
                                                w_sb[:, 0, k], start=(k == 0), stop=(k == KC - 1))
                last.then_inc(y_summed, 1)

            def dense(dit, jd):
                n = dense_nodes(dit * 2 + jd)
                if n:
                    turn_x(dit, jd, n)
                    sum_y(dit, jd, n)

            def sort_pass(n, width):
                for it in (0, None):
                    if it == 0:
                        for j in range(UNROLL):
                            count(n * PH, j, width, True)
                    else:
                        with pe.Fori(n * PH + 1, (n + 1) * PH) as it:
                            for j in range(UNROLL):
                                count(it, j, width, False)
                pe.wait_ge(counts_read, n + 1)
                nc.tensor.matmul(ps_h[1].rearrange("p k n -> p (k n)")[:, 0:width], ones[:], counts[:, 0:width],
                                 start=True, stop=True)
                nc.tensor.matmul(ps_r[1].rearrange("p k n -> p (k n)")[:, 0:width], below[:], counts[:, 0:width],
                                 start=True, stop=True).then_inc(based, 1)

            def count(it, j, width, first):
                t = it * UNROLL + j
                pe.wait_ge(hot_built, t + 1)
                nc.tensor.matmul(ps_h[0].rearrange("p k n -> p (k n)")[:, 0:width], ident_b[:],
                                 hot[:, j, 0:width], start=first and j == 0,
                                 stop=True, skip_group_check=True).then_inc(hot_used, 1)

            for n, width in ((0, LO), (1, HI)):
                sort_pass(n, width)
                if n == 0:
                    dense(0, 0)
                    dense(0, 1)
                with pe.Fori(n * PH + (n == 0), (n + 1) * PH) as it:
                    dense(it, 0)
                    dense(it, 1)

            pe.wait_ge(cols_f, 2)
            pe.wait_ge(xT_ready, 2 * ITS)
            for half in range(2):
                for n, a in enumerate((col_r, tidx_r, row_r, val_r)):
                    last = nc.tensor.transpose(ps_x[half][:, n, 0:EROWS], a[:, half * P:(half + 1) * P],
                                               ident[0:EROWS, 0:EROWS])
            last.then_inc(meta_turned, 1)
            pe.wait_ge(meta_ready, 1)

            def turn_h(it, j):
                t = it * UNROLL + j
                b = (j - 1) % 2
                pe.wait_ge(hT_ready, t)
                at_least(pe, h_row_ready, t - 2)
                for k in range(KC):
                    last = nc.tensor.transpose(ps_r[b][:, k], hT[:, (j - 1) % UNROLL, k], ident[:])
                last.then_inc(h_turned, 1)

            def sum_h(it, j):
                t = it * UNROLL + j
                pe.wait_ge(g_landed[j], 16 * uses(it, j))
                pe.wait_ge(s_built, t + 1)
                at_least(pe, hT_ready, t - 1)
                for k in range(KC):
                    last = nc.tensor.matmul(ps_h[j % 2][:, k], gath[:, j, k * P:(k + 1) * P], S[:, j],
                                            start=True, stop=True)
                last.then_inc(h_summed, 1)

            def step(it, j, behind=True):
                n = dense_nodes((it + ITS) * 2 + j // 2)
                if n and j % 2 == 0:
                    turn_x(it + ITS, j // 2, n)
                if n and j % 2:
                    sum_y(it + ITS, j // 2, n)
                if behind:
                    turn_h(it, j)
                sum_h(it, j)

            for j in range(UNROLL):
                step(0, j, j > 0)
            with pe.Fori(1, ITS - 1) as it:
                for j in range(UNROLL):
                    step(it, j)
            for j in range(UNROLL):
                step(ITS - 1, j)
            turn_h(ITS, 0)

            pe.wait_ge(xT_ready, DENSE + 1)
            pe.wait_ge(h_row_ready, STEPS)
            pe.wait_ge(hT_ready, STEPS)
            pe.wait_ge(y1_ready, DENSE + 1)

            def turn_all(it, j):
                i = it * UNROLL + j
                b = j % 2
                pe.wait_ge(c_x_landed[j], 16 * uses(it, j))
                pe.wait_ge(c_h_landed[j], 2 * 16 * uses(it, j))
                at_least(pe, c_T_ready, i - 1)
                for k in range(KC):
                    cols = slice(k * P, (k + 1) * P)
                    nc.tensor.transpose(ps_x[b][:, k], x_dst[:, j, cols], ident[:])
                    nc.tensor.transpose(ps_x[b][:, KC + k], h_in[:, j, 0, cols], ident[:])
                    last = nc.tensor.transpose(ps_r[b][:, k], h_in[:, j, 1, cols], ident[:])
                last.then_inc(c_turned, 1)

            def sum_h3(it, j):
                i = it * UNROLL + j
                pe.wait_ge(c_g_landed[j], 16 * uses(it, j))
                pe.wait_ge(c_s_built, i + 1)
                at_least(pe, c_hT_ready, i - 1)
                for k in range(KC):
                    last = nc.tensor.matmul(ps_h[j % 2][:, k], gath[:, j, k * P:(k + 1) * P], S[:, j],
                                            start=True, stop=True)
                last.then_inc(c_h_summed, 1)

            def sum_all(it, j):
                i = it * UNROLL + j
                b, slot = (j - 1) % 2, (j - 1) % UNROLL
                pe.wait_ge(c_T_ready, i)
                pe.wait_ge(c_hT_ready, i)
                at_least(pe, c_ready, i - 2)
                for h in range(HOPS + 1):
                    for k in range(KC):
                        lhsT = cT[:, slot, KC * h + k] if h < HOPS else hT[:, slot, k]
                        last = nc.tensor.matmul(ps_y[b][:, 0], lhsT, w_sb[:, h, k],
                                                start=(h == 0 and k == 0), stop=(h == HOPS and k == KC - 1))
                last.then_inc(c_y_summed, 1)

            for j in range(UNROLL):
                turn_all(0, j)
                sum_h3(0, j)
                if j:
                    sum_all(0, j)
            with pe.Fori(1, PH) as it:
                for j in range(UNROLL):
                    turn_all(it, j)
                    sum_h3(it, j)
                    sum_all(it, j)
            sum_all(PH, 0)

        @block.scalar
        def _(act):
            def put_xT(dit, jd, n=P):
                d = dit * 2 + jd
                act.wait_ge(x_turned, d + 1)
                at_least(act, y_summed, d - 1)
                nc.scalar.activation(xT[:, jd].rearrange("p r k n -> p (r k) n")[:, :, 0:n],
                                     ps_x[jd][:, :, 0:n], ACT.Copy).then_inc(xT_ready, 1)

            def put_h_row(it, j):
                t = it * UNROLL + j
                slot = (j - 1) % UNROLL
                act.wait_ge(h_turned, t)
                at_least(act, h_stored[slot], 16 * (uses(it, j, -1) - 1))
                nc.scalar.activation(h_row[:, slot], ps_r[(j - 1) % 2][:, 0:KC].rearrange("p k n -> p (k n)"),
                                     ACT.Copy).then_inc(h_row_ready, 1)

            def norm(dit, jd, n=P):
                d = dit * 2 + jd
                act.wait_ge(mv_ready, d + 1)
                nc.scalar.activation(std[0:n, jd], mv[0:n, jd, :, 1], ACT.Sqrt, bias=eps[0:n]).then_inc(std_ready, 1)
                act.wait_ge(y0_ready, d + 1)
                at_least(act, y_stored[jd], 16 * dit)
                nc.scalar.activation(y_out[0:n, jd, 1], ps_y[jd][0:n, 1], ACT.Identity,
                                     bias=nmr[0:n, jd], scale=rstd[0:n, jd, 1:2]).then_inc(y1_ready, 1)

            def dense(dit, jd):
                n = dense_nodes(dit * 2 + jd)
                if n:
                    put_xT(dit, jd, n)
                    norm(dit, jd, n)

            act.wait_ge(setup_done, 1)
            dense(0, 0)
            dense(0, 1)
            with act.Fori(1, ITS) as it:
                dense(it, 0)
                dense(it, 1)

            def step(it, j, behind=True):
                n = dense_nodes((it + ITS) * 2 + j // 2)
                if n and j % 2 == 0:
                    put_xT(it + ITS, j // 2, n)
                if behind:
                    put_h_row(it, j)
                if n and j % 2:
                    norm(it + ITS, j // 2, n)

            for j in range(UNROLL):
                step(0, j, j > 0)
            with act.Fori(1, ITS - 1) as it:
                for j in range(UNROLL):
                    step(it, j)
            for j in range(UNROLL):
                step(ITS - 1, j)
            put_h_row(ITS, 0)

            def put_cT(it, j):
                i = it * UNROLL + j
                act.wait_ge(c_turned, i + 1)
                at_least(act, c_y_summed, i - UNROLL + 1)
                nc.scalar.activation(cT[:, j, 0:4], ps_x[j % 2][:], ACT.Copy)
                nc.scalar.activation(cT[:, j, 4:6], ps_r[j % 2][:, 0:KC], ACT.Copy).then_inc(c_T_ready, 1)

            def c_std(it, j):
                i = it * UNROLL + j
                b = (j - 1) % 2
                act.wait_ge(c_mv_ready, i)
                nc.scalar.activation(std[:, b, 0:1], mv[:, b, 0, 1:2], ACT.Sqrt, bias=eps[:]).then_inc(c_std_ready, 1)

            for j in range(UNROLL):
                put_cT(0, j)
                if j:
                    c_std(0, j)
            with act.Fori(1, PH) as it:
                for j in range(UNROLL):
                    put_cT(it, j)
                    c_std(it, j)
            c_std(PH, 0)

        @block.vector
        def _(dve):
            nc.vector.memset(row_in[:], PAD_ROW)
            nc.vector.memset(col_in[:], 0)
            nc.vector.memset(val_in[:], 0.0)
            nc.vector.memset(before[:], -2.0)
            nc.vector.memset(nowhere[:], NOWHERE).then_inc(pads_set, 1)
            nc.vector.memset(eps[:], EPS)
            nc.vector.memset(ones_w[:], 1.0)
            nc.vector.memset(rec[:], 0)
            nc.vector.memset(next_r[:], PAD_ROW)
            nc.vector.memset(meta[:], 0).then_inc(meta_cleared, 1)
            dve.wait_ge(counter_set, 1)
            nc.vector.tensor_copy(counter[:], counter_i[:])
            nc.vector.tensor_copy(counter_h[:], counter_i[:]).then_inc(counter_set, 1)
            dve.wait_ge(consts_set, 2)
            nc.vector.tensor_copy(ident_b[:], ident[:])
            dve.wait_ge(w_in, 16)
            nc.vector.tensor_copy(w_sb[:].rearrange("p h k o -> p k o h"),
                                  w_raw[:].rearrange("p k (o h) -> p k o h", h=HOPS + 1)).then_inc(w_split, 1)
            dve.wait_ge(w_split, 1)
            for k in range(KC):
                block_k = w_sb[:, 0, k, k * P:(k + 1) * P]
                last = nc.vector.tensor_tensor(block_k, block_k, ident[:], ALU.add)
            last.then_inc(setup_done, 1)
            dve.wait_ge(edges_in, 6 * 16)
            dve.wait_ge(meta_cleared, 1)
            nc.vector.tensor_copy(rec[:, :, 0], row_in[:])
            nc.vector.tensor_copy(rec[:, :, 1], col_in[:])
            nc.vector.tensor_copy(rec[:, :, 2].bitcast(F32), val_in[:]).then_inc(digits_set, 1)
            dve.wait_ge(counter_set, 2)
            dve.wait_ge(digits_set, 1)

            def digits(n):
                if n == 0:
                    nc.vector.tensor_scalar(digit_i[:], rec[:, :, 0], LO - 1, None, ALU.bitwise_and
                                            ).then_inc(digits_set, 1)
                else:
                    nc.vector.tensor_scalar(digit_i[:], rec[:, :, 0], LO.bit_length() - 1, None,
                                            ALU.logical_shift_right).then_inc(digits_set, 1)
                dve.wait_ge(digits_set, 2 * n + 2)
                nc.vector.tensor_copy(digit[:], digit_i[:]).then_inc(digits_set, 1)
                dve.wait_ge(digits_set, 2 * n + 3)

            def one_hot(it, n, j, width):
                t = it * UNROLL + j
                at_least(dve, hot_used, t - UNROLL + 1)
                nc.vector.tensor_scalar(hot[:, j, 0:width], counter_h[:, 0:width],
                                        digit[:, bass.ds(t - n * TILES, 1)], None, ALU.is_equal
                                        ).then_inc(hot_built, 1)

            def first_places(n, width):
                dve.wait_ge(hot_used, (n + 1) * TILES)
                nc.vector.tensor_copy(counts[:, 0:width], ps_h[0].rearrange("p k n -> p (k n)")[:, 0:width]
                                      ).then_inc(counts_read, 1)
                dve.wait_ge(based, n + 1)
                total = ps_h[1].rearrange("p k n -> p (k n)")[:, 0:width]
                lower = ps_r[1].rearrange("p k n -> p (k n)")[:, 0:width]
                nc.vector.tensor_tensor_scan(upto[:, 0:width], ones_w[:, 0:width], total, 0.0,
                                             ALU.mult, ALU.add).then_inc(upto_set, 1)
                dve.wait_ge(upto_set, 2 * n + 1)
                nc.vector.tensor_tensor(upto[:, 0:width], upto[:, 0:width], total, ALU.subtract).then_inc(upto_set, 1)
                dve.wait_ge(upto_set, 2 * n + 2)
                nc.vector.tensor_tensor(place[:, 0:width], upto[:, 0:width], lower, ALU.add).then_inc(place_set, 1)
                dve.wait_ge(place_set, n + 1)

            def sort(it, n, j, width, measured=False):
                t = it * UNROLL + j
                d_t = digit[:, bass.ds(t - n * TILES, 1)]
                at_least(dve, rec_landed[j], 16 * it)
                at_least(dve, place_moved, t)
                nc.vector.scalar_tensor_tensor(picked[:, 0:width], counter[:, 0:width], d_t, place[:, 0:width],
                                               ALU.is_equal, ALU.mult, accum_out=place_f[:, j:j + 1])
                nc.vector.scalar_tensor_tensor(place[:, 0:width], counter[:, 0:width], d_t, place[:, 0:width],
                                               ALU.is_equal, ALU.add).then_inc(place_moved, 1)
                nc.vector.tensor_scalar(rec_out[:, j], rec[:, bass.ds(t - n * TILES, 1)].rearrange("p o w -> p (o w)"),
                                        0, None, ALU.bitwise_or)
                dve.wait_ge(place_moved, t + 1)
                nc.vector.tensor_copy(rec_idx[:, j:j + 1], place_f[:, j:j + 1]).then_inc(rec_staged, 1)

            def measure(dit, jd, n=P):
                d = dit * 2 + jd
                dve.wait_ge(y_summed, d + 1)
                for r in range(2):
                    last = nc.vector.bn_stats(stats[0:n, jd, r], ps_y[jd][0:n, r])
                last.then_inc(stats_ready, 1)
                dve.wait_ge(stats_ready, d + 1)

            def mean_variance(jd, n=P):
                for r in range(2):
                    last = nc.vector.bn_aggr(mv[0:n, jd, r], stats[0:n, jd, r])
                last.then_inc(mv_ready, 1)

            def norm(dit, jd, n=P):
                d = dit * 2 + jd
                dve.wait_ge(std_ready, d + 1)
                nc.vector.reciprocal(rstd[0:n, jd], std[0:n, jd]).then_inc(rstd_ready, 1)
                dve.wait_ge(rstd_ready, d + 1)
                nc.vector.scalar_tensor_tensor(nmr[0:n, jd], mv[0:n, jd, 1, 0:1], -1.0, rstd[0:n, jd, 1:2],
                                               ALU.mult, ALU.mult)
                at_least(dve, y_stored[jd], 16 * dit)
                nc.vector.tensor_scalar(y_out[0:n, jd, 0], ps_y[jd][0:n, 0], mv[0:n, jd, 0, 0:1],
                                        rstd[0:n, jd, 0:1], ALU.subtract, ALU.mult).then_inc(y0_ready, 1)

            def sort_four(it, n, width):
                for j in range(UNROLL):
                    if j % 2:
                        measure(it, j // 2)
                    sort(it, n, j, width)
                    if j % 2:
                        mean_variance(j // 2)
                        norm(it, j // 2)

            for n, width in ((0, LO), (1, HI)):
                if n:
                    dve.wait_ge(by_lo_in, 16)
                digits(n)
                if n == 0:
                    for j in range(UNROLL):
                        one_hot(0, n, j, width)
                with dve.Fori(n * PH + (n == 0), (n + 1) * PH) as it:
                    for j in range(UNROLL):
                        one_hot(it, n, j, width)
                first_places(n, width)
                if n == 0:
                    sort_four(0, n, width)
                with dve.Fori(n * PH + (n == 0), (n + 1) * PH) as it:
                    sort_four(it, n, width)

            nc.vector.memset(hT[:], 0.0)
            nc.vector.memset(x_dst[:], 0.0).then_inc(meta_cleared, 1)
            dve.wait_ge(by_row_in, 3 * 16)
            nc.vector.tensor_copy(row_r[:], rec_r[:, :, 0]).then_inc(cols_f, 1)
            nc.vector.tensor_copy(col_r[:], rec_r[:, :, 1])
            nc.vector.tensor_copy(val_r[:], rec_r[:, :, 2].bitcast(F32))
            nc.vector.tensor_tensor(last_r[:], rec_r[:, :, 0], next_r[:, :, 0], ALU.not_equal).then_inc(last_set, 1)
            dve.wait_ge(last_set, 1)
            nc.vector.scalar_tensor_tensor(tidx_r[:], row_r[:], float(-NOWHERE), last_r[:],
                                           ALU.add, ALU.mult).then_inc(shifted, 1)
            dve.wait_ge(shifted, 1)
            nc.vector.tensor_scalar(tidx_r[:], tidx_r[:], float(NOWHERE), None, ALU.add).then_inc(cols_f, 1)
            dve.wait_ge(meta_turned, 1)
            dve.wait_ge(places_set, 1)
            dve.wait_ge(meta_cleared, 2)
            for half in range(2):
                tiles = slice(half, TILES, 2)
                nc.vector.tensor_copy(meta[:, tiles, 0], ps_x[half][:, 0, 0:EROWS])
                nc.vector.tensor_copy(meta[:, tiles, 1], ps_x[half][:, 1, 0:EROWS])
                for k in range(2):
                    nc.vector.tensor_copy(d_col[:, slice(half + k * TILES, (k + 1) * TILES, 2)],
                                          ps_x[half][:, 2, 0:EROWS])
                last = nc.vector.tensor_copy(w_col[:, tiles], ps_x[half][:, 3, 0:EROWS])
            last.then_inc(meta_ready, 1)
            dve.wait_ge(meta_ready, 1)

            def stage(it, j):
                t = it * UNROLL + j
                at_least(dve, g_landed[j], 16 * (uses(it, j) - 1))
                at_least(dve, t_landed[j], 16 * (uses(it, j) - 1))
                nc.vector.tensor_copy(a_idx[:, j], meta[:, bass.ds(t, 1), 0:3].rearrange("p o n -> p (o n)")
                                      ).then_inc(staged, 1)

            def ask_later(t, j):
                nc.vector.tensor_copy(q_src[:, j:j + 1], meta[:, bass.ds(t - TILES, 1), 0]).then_inc(q_used, 1)

            def use_place(it, j):
                t = it * UNROLL + j
                dve.wait_ge(q_landed[j], 16 * (uses(it, j) - PH))
                nc.vector.scalar_tensor_tensor(w_col[:, bass.ds(t, 1)], q_got[:, j:j + 1], float(E_PAD),
                                               w_col[:, bass.ds(t - TILES, 1)], ALU.is_lt, ALU.mult)
                nc.vector.tensor_copy(h_idx[:, j:j + 1], q_got[:, j:j + 1])
                nc.vector.tensor_copy(meta[:, bass.ds(t - TILES, 1), 3], q_got[:, j:j + 1])
                ask_later(t + UNROLL, j)

            def build(it, j, col, landed, done, places, between=None):
                half = j // 2
                dve.wait_ge(landed[half], 16 * (it + 1))
                if places is not None:
                    dve.wait_ge(q_used, places)
                line = dst_b[:, half, 1 + (j % 2) * P:1 + (j % 2 + 1) * P]
                nc.vector.tensor_scalar(S[:, j], line, d_col[:, bass.ds(col, 1)], w_col[:, bass.ds(col, 1)],
                                        ALU.is_equal, ALU.mult)
                if between:
                    between()
                nc.vector.tensor_scalar(same[:, j], line, dst_b[:, half, (j % 2) * P:(j % 2) * P + 1], None,
                                        ALU.is_equal).then_inc(done, 1)

            def carry(t, j, summed, built, ready):
                dve.wait_ge(summed, t + 1)
                dve.wait_ge(built, t + 1)
                at_least(dve, ready, t)
                for k in range(KC):
                    last = nc.vector.scalar_tensor_tensor(
                        hT[:, j, k], same[:, j], hT[:, (j - 1) % UNROLL, k, P - 1:P], ps_h[j % 2][:, k],
                        ALU.mult, ALU.add)
                last.then_inc(ready, 1)

            def step(it, j, hop, stages=True):
                t = it * UNROLL + j
                n = dense_nodes((it + ITS) * 2 + j // 2) if j % 2 else 0
                if hop == 1:
                    stage(it + (j + 3) // UNROLL, (j + 3) % UNROLL)
                elif stages:
                    use_place(it + (j + 3) // UNROLL, (j + 3) % UNROLL)
                build(it, j, t, dst_landed, s_built, None if hop == 1 else t - TILES + UNROLL + 1,
                      (lambda: measure(it + ITS, j // 2, n)) if n else None)
                if n:
                    mean_variance(j // 2, n)
                at_least(dve, h_turned, t - UNROLL + 1)
                carry(t, j, h_summed, s_built, hT_ready)
                if n:
                    norm(it + ITS, j // 2, n)

            for j in range(UNROLL - 1):
                stage(0, j)
            for j in range(UNROLL):
                step(0, j, 1)
            with dve.Fori(1, PH) as it:
                for j in range(UNROLL):
                    step(it, j, 1)
            for j in range(UNROLL):
                ask_later(TILES + j, j)
            for j in range(UNROLL - 1):
                use_place(PH, j)
            with dve.Fori(PH, ITS - 1) as it:
                for j in range(UNROLL):
                    step(it, j, 2)
            for j in range(UNROLL):
                step(ITS - 1, j, 2, j == 0)

            def c_stage(it, j):
                at_least(dve, c_x_landed[j], 16 * (uses(it, j) - 1))
                at_least(dve, c_g_landed[j], 16 * (uses(it, j) - 1))
                nc.vector.tensor_copy(c_idx[:, j], meta[:, bass.ds(it * UNROLL + j, 1), 1:4].rearrange(
                    "p o n -> p (o n)")).then_inc(c_staged, 1)

            def c_measure(it, j):
                i = it * UNROLL + j
                b, slot = (j - 1) % 2, (j - 1) % UNROLL
                dve.wait_ge(c_y_summed, i)
                nc.vector.bn_stats(stats[:, b, 0], ps_y[b][:, 0]).then_inc(c_stats_ready, 1)
                at_least(dve, c_stored[slot], 16 * (uses(it, j, -1) - 1))
                dve.wait_ge(c_stats_ready, i)
                nc.vector.tensor_copy(o_idx[:, slot:slot + 1], meta[:, bass.ds(i - 1, 1), 1]).then_inc(c_out_staged, 1)
                nc.vector.bn_aggr(mv[:, b, 0], stats[:, b, 0]).then_inc(c_mv_ready, 1)

            def c_norm(it, j):
                i = it * UNROLL + j
                b, slot = (j - 1) % 2, (j - 1) % UNROLL
                dve.wait_ge(c_std_ready, i)
                nc.vector.reciprocal(rstd[:, b, 0:1], std[:, b, 0:1]).then_inc(c_rstd_ready, 1)
                dve.wait_ge(c_rstd_ready, i)
                nc.vector.tensor_scalar(res[:, slot], ps_y[b][:, 0], mv[:, b, 0, 0:1], rstd[:, b, 0:1],
                                        ALU.subtract, ALU.mult).then_inc(c_ready, 1)

            def finish(it, j, behind=True):
                i = it * UNROLL + j
                c_stage(it + (j + 3) // UNROLL, (j + 3) % UNROLL)
                build(it, j, i + TILES, c_dst_landed, c_s_built, None)
                at_least(dve, c_y_summed, i - UNROLL + 1)
                carry(i, j, c_h_summed, c_s_built, c_hT_ready)
                if behind:
                    c_measure(it, j)
                    c_norm(it, j)

            dve.wait_ge(q_used, TILES + 1)
            for j in range(UNROLL - 1):
                c_stage(0, j)
            for j in range(UNROLL):
                finish(0, j, j > 0)
            with dve.Fori(1, PH) as it:
                for j in range(UNROLL):
                    finish(it, j)
            c_measure(PH, 0)
            c_norm(PH, 0)


_INS = ['x', 'src', 'dst', 'edge_weight', 'L0_gnn_weight']


def kernel(**inputs):
    import numpy as _np
    import concourse.bacc as _bacc
    from concourse import mybir as _mybir
    from concourse.bass_utils import run_bass_kernel_spmd as _run

    nc = _bacc.Bacc("TRN2", target_bir_lowering=False, num_devices=1)
    arrays, args = {}, []
    for name in _INS:
        a = _np.ascontiguousarray(inputs[name])
        arrays[f"in_{name}_dram"] = a
        args.append(nc.dram_tensor(f"in_{name}_dram", a.shape, _mybir.dt.from_np(a.dtype), kind="ExternalInput").ap())
    shape = inputs['x'].shape
    args.append(nc.dram_tensor("out_0_dram", shape, _mybir.dt.float32, kind="ExternalOutput").ap())
    gnn_program(nc, *args)
    r = _run(nc, [arrays], core_ids=[0])
    return r.results[0]["out_0_dram"]
```

```python
from contextlib import ExitStack

import concourse.bass as bass
from concourse import mybir

P = 128
F32 = mybir.dt.float32
F16 = mybir.dt.float16
BF16 = mybir.dt.bfloat16
I32 = mybir.dt.int32
ALU = mybir.AluOpType
ACT = mybir.ActivationFunctionType

EPS = 1e-5
UNROLL = 4
NOWHERE = 1 << 20


def step_done(eng, sems, it, j, back=0, by=1):
    times = it + (j - back) // len(sems) + 1
    if isinstance(times, int) and times <= 0:
        return
    eng.wait_ge(sems[(j - back) % len(sems)], times * by)


def gnn_program(nc, x, row, col, value, weight, out):
    N, C = x.shape
    E = row.shape[0]
    CO = weight.shape[1]
    HOPS = weight.shape[2] - 1
    KC = C // P
    TILES = -(-E // (P * UNROLL)) * UNROLL
    E_PAD = TILES * P
    STEPS = 2 * TILES
    ITS = STEPS // UNROLL
    PH = TILES // UNROLL
    ROWS = 2 * P
    DENSE = N // ROWS
    TAIL = N - DENSE * ROWS
    TAIL_P = TAIL // 2
    META = TILES + UNROLL
    NT = -(-N // P)
    EROWS = TILES // 2
    LO = 256
    HI = N // LO + 2
    PAD_ROW = (HI - 1) * LO
    REC = 4
    FITS = ITS + PH
    DITS = 2 * ITS
    assert C == 2 * P and CO == 2 * P and HOPS == 3 and TILES % UNROLL == 0
    assert 2 * (DITS - 1) <= DENSE < 2 * DITS - 1 and TAIL % 2 == 0 and 0 < TAIL_P <= P
    assert N <= PAD_ROW < NOWHERE and LO <= 512 and HI <= 512

    h1_rows = nc.dram_tensor("h1_rows", (E_PAD, C), F32, kind="Internal").ap()
    h2_rows = nc.dram_tensor("h2_rows", (E_PAD, C), F32, kind="Internal").ap()
    place_of = nc.dram_tensor("place_of", (NT * P, 1), I32, kind="Internal").ap()
    h2_cols = nc.dram_tensor("h2_cols", (E_PAD, C), F32, kind="Internal").ap()
    by_lo = nc.dram_tensor("by_lo", (E_PAD, REC), I32, kind="Internal").ap()
    by_row = nc.dram_tensor("by_row", (E_PAD, REC), I32, kind="Internal").ap()
    row_line = nc.dram_tensor("row_line", (E_PAD,), F32, kind="Internal").ap()

    with ExitStack() as ctx:
        def sb(name, shape, dt=F32):
            return ctx.enter_context(nc.sbuf_tensor(name, shape, dt))

        def sem(name):
            return ctx.enter_context(nc.semaphore(name))

        def sems(name, n=UNROLL):
            return [sem(f"{name}{i}") for i in range(n)]

        ident = sb("ident", [P, P])
        w_raw = sb("w_raw", [P, KC, CO * (HOPS + 1)])
        w_sb = sb("w_sb", [P, HOPS + 1, KC, CO])
        eps = sb("eps", [P, 1])
        ident_b = sb("ident_b", [P, P], BF16)
        ones = sb("ones", [P, P])
        below = sb("below", [P, P])
        counter_i = sb("counter_i", [P, HI], I32)
        counter = sb("counter", [P, HI])
        counter_h = sb("counter_h", [P, HI], F16)
        row_in = sb("row_in", [P, TILES], I32)
        col_in = sb("col_in", [P, TILES], I32)
        val_in = sb("val_in", [P, TILES])
        rec = sb("rec", [P, TILES, REC], I32)
        digit_i = sb("digit_i", [P, TILES], I32)
        digit = sb("digit", [P, TILES])
        hot = sb("hot", [P, UNROLL, HI], BF16)
        counts = sb("counts", [P, HI])
        upto = sb("upto", [P, HI])
        ones_w = sb("ones_w", [P, HI])
        place = sb("place", [P, HI])
        picked = sb("picked", [P, HI])
        place_f = sb("place_f", [P, UNROLL])
        rec_idx = sb("rec_idx", [P, UNROLL], I32)
        rec_out = sb("rec_out", [P, UNROLL, REC], I32)
        rec_r = sb("rec_r", [EROWS, 2 * P, REC], I32)
        next_r = sb("next_r", [EROWS, 2 * P, REC], I32)
        val_r = sb("val_r", [EROWS, 2 * P])
        col_r = sb("col_r", [EROWS, 2 * P])
        row_r = sb("row_r", [EROWS, 2 * P])
        last_r = sb("last_r", [EROWS, 2 * P])
        tidx_r = sb("tidx_r", [EROWS, 2 * P])
        nowhere = sb("nowhere", [P, NT], I32)
        meta = sb("meta", [P, META, 4], I32)
        r_col = sb("r_col", [P, TILES])
        v_col = sb("v_col", [P, STEPS])
        a_idx = sb("a_idx", [P, UNROLL, 3], I32)
        q_src = sb("q_src", [P, UNROLL], I32)
        q_got = sb("q_got", [P, UNROLL], I32)
        h_idx = sb("h_idx", [P, UNROLL], I32)
        c_idx = sb("c_idx", [P, UNROLL, 3], I32)
        o_idx = sb("o_idx", [P, UNROLL], I32)
        row_b = sb("row_b", [P, 1 + E_PAD])
        gath = sb("gath", [P, UNROLL, C])
        S = sb("S", [P, UNROLL, P])
        same = sb("same", [P, UNROLL, P])
        hT = sb("hT", [P, UNROLL, KC, P])
        h_row = sb("h_row", [P, UNROLL, C])
        x_in = sb("x_in", [P, 2, 2, C])
        xT = sb("xT", [P, 2, 2, KC, P])
        stats = sb("stats", [P, 2, 2, 6])
        mv = sb("mv", [P, 2, 2, 2])
        std = sb("std", [P, 2, 2])
        rstd = sb("rstd", [P, 2, 2])
        nmr = sb("nmr", [P, 2, 2])
        y_out = sb("y_out", [P, 2, 2, CO])
        x_dst = sb("x_dst", [P, UNROLL, C])
        h1_in = x_in[:].rearrange("p d r c -> p (d r) c")
        h2T_in = xT[:].rearrange("p d r k n -> p (d r) k n")
        cT = w_raw[:].rearrange("p k (a n q) -> p (k a) n q", a=2, q=P)
        res = y_out[:].rearrange("p d r c -> p (d r) c")

        ps_x = [ctx.enter_context(nc.psum_tensor(f"ps_x{i}", [P, 4, P], F32)) for i in range(2)]
        ps_y = [ctx.enter_context(nc.psum_tensor(f"ps_y{i}", [P, 2, CO], F32)) for i in range(2)]
        ps_h = [ctx.enter_context(nc.psum_tensor(f"ps_h{i}", [P, 4, P], F32)) for i in range(2)]
        ps_r = [ctx.enter_context(nc.psum_tensor(f"ps_r{i}", [P, 4, P], F32)) for i in range(2)]

        pads_set = sem("pads_set")
        edges_in = sem("edges_in")
        w_in = sem("w_in")
        consts_set = sem("consts_set")
        counter_set = sem("counter_set")
        digits_set = sem("digits_set")
        hot_built = sems("hot_built")
        hot_used = sems("hot_used")
        counts_read = sem("counts_read")
        based = sem("based")
        upto_set = sem("upto_set")
        place_moved = sems("place_moved")
        rec_staged = sems("rec_staged")
        rec_landed = sems("rec_landed")
        records_in = sem("records_in")
        cols_f = sem("cols_f")
        line_out = sem("line_out")
        table_out = sem("table_out")
        shifted = sem("shifted")
        meta_turned = sem("meta_turned")
        meta_cleared = sem("meta_cleared")
        places_set = sem("places_set")
        setup_done = sem("setup_done")
        meta_ready = sem("meta_ready")
        pool_goes = sem("pool_goes")
        x_landed = sems("x_landed", 2)
        y_stored = sems("y_stored", 2)
        row_landed = sems("row_landed", 2)
        g_landed = sems("g_landed")
        t_landed = sems("t_landed")
        q_landed = sems("q_landed")
        h_stored = sems("h_stored")
        hT_stored = sems("hT_stored")
        x_turned = sems("x_turned", 2)
        xT_ready = sems("xT_ready", 2)
        y_summed = sems("y_summed", 2)
        stats_ready = sems("stats_ready", 2)
        mv_ready = sems("mv_ready", 2)
        std_ready = sems("std_ready", 2)
        rstd_ready = sems("rstd_ready", 2)
        nmr_ready = sems("nmr_ready", 2)
        y_ready = sems("y_ready", 2)
        staged = sems("staged")
        q_used = sems("q_used")
        s_built = sems("s_built")
        h_summed = sems("h_summed")
        hT_ready = sems("hT_ready")
        h_turned = sems("h_turned")
        h_row_ready = sems("h_row_ready")
        c_h_landed = sems("c_h_landed")
        c_x_landed = sems("c_x_landed")
        c_stored = sems("c_stored")
        c_staged = sems("c_staged")
        c_y_summed = sems("c_y_summed")
        c_stats_ready = sems("c_stats_ready")
        c_mv_ready = sems("c_mv_ready")
        c_std_ready = sems("c_std_ready")
        c_rstd_ready = sems("c_rstd_ready")
        c_nmr_ready = sems("c_nmr_ready")
        c_ready = sems("c_ready")

        def dense_nodes(d):
            return P if not isinstance(d, int) or d < DENSE else TAIL_P if d == DENSE else 0

        def dense_rows(a, t):
            return a[bass.ds(t * ROWS, ROWS), :].rearrange("(p r) c -> p r c", r=2)

        def tail_of(a):
            return a[DENSE * ROWS:N, :].rearrange("(p r) c -> p r c", r=2)

        block = ctx.enter_context(nc.Block())

        @block.sync
        def _(sp):
            sp.wait_ge(pads_set, 1)
            full = E // TILES
            for tile, a in ((row_in, row), (col_in, col), (val_in, value)):
                sp.dma_start(tile[0:full, :], a[0:full * TILES].rearrange("(p t) -> p t", t=TILES)
                             ).then_inc(edges_in, 16)
                sp.dma_start(tile[full:full + 1, 0:E - full * TILES],
                             a[full * TILES:E].rearrange("(o n) -> o n", o=1)).then_inc(edges_in, 16)
            sp.dma_start(w_raw[:], weight.rearrange("(k p) o h -> p k (o h)", p=P)).then_inc(w_in, 16)
            for d in range(2):
                sp.dma_start(x_in[:, d], dense_rows(x, d)).then_inc(x_landed[d], 16)
            sp.dma_start(place_of.rearrange("(p t) o -> p (t o)", p=P), nowhere[:]).then_inc(table_out, 16)

            def dense(dit, jd):
                d = dit * 2 + jd
                fixed = isinstance(d, int)
                slot = (jd + 1) % 2
                if (not fixed or d + 1 <= DENSE) and not (fixed and d == 0):
                    step_done(sp, x_turned, dit, jd, 1)
                    if fixed and d + 1 == DENSE:
                        sp.dma_start(x_in[0:TAIL_P, slot], tail_of(x)).then_inc(x_landed[slot], 16)
                    else:
                        sp.dma_start(x_in[:, slot], dense_rows(x, d + 1)).then_inc(x_landed[slot], 16)
                if not fixed or d > 0:
                    step_done(sp, y_ready, dit, jd, 1)
                    if fixed and d - 1 == DENSE:
                        sp.dma_start(tail_of(out), y_out[0:TAIL_P, slot]).then_inc(y_stored[slot], 16)
                    else:
                        sp.dma_start(dense_rows(out, d - 1), y_out[:, slot]).then_inc(y_stored[slot], 16)

            dense(0, 0)
            dense(0, 1)
            with sp.Fori(1, PH) as it:
                dense(it, 0)
                dense(it, 1)
            for j in range(UNROLL):
                sp.wait_ge(rec_landed[j], 16 * PH)
            sp.dma_start(rec[:], by_lo.rearrange("(p t) w -> p t w", t=TILES)).then_inc(records_in, 16)
            with sp.Fori(PH, ITS) as it:
                dense(it, 0)
                dense(it, 1)
            for j in range(UNROLL):
                sp.wait_ge(rec_landed[j], 16 * ITS)
            sp.dma_start(rec_r[:], by_row.rearrange("(r n) w -> r n w", n=2 * P)).then_inc(records_in, 16)
            sp.dma_start(next_r[0:EROWS - 1], by_row[1:1 + (EROWS - 1) * 2 * P, :].rearrange(
                "(r n) w -> r n w", n=2 * P)).then_inc(records_in, 16)
            sp.dma_start(next_r[EROWS - 1:EROWS, 0:2 * P - 1], by_row[1 + (EROWS - 1) * 2 * P:E_PAD, :].rearrange(
                "(o n) w -> o n w", o=1)).then_inc(records_in, 16)
            sp.wait_ge(cols_f, 1)
            sp.dma_start(row_line.rearrange("(r n) -> r n", n=2 * P), row_r[:]).then_inc(line_out, 16)
            sp.wait_ge(line_out, 16)

            def load_rows(pair, half):
                sp.dma_start(row_b[:, bass.ds(1 + pair * 2 * P, 2 * P)],
                             row_line[bass.ds(pair * 2 * P, 2 * P)].rearrange("(o n) -> o n", o=1).broadcast_to((P, 2 * P))
                             ).then_inc(row_landed[half], 16)

            load_rows(0, 0)
            load_rows(1, 1)

            def step(it, j, hop, rows_too=True):
                t = it * UNROLL + j
                if j % 2 == 0:
                    dense(it + ITS, j // 2)
                    if hop == 1 and rows_too:
                        step_done(sp, row_landed, it, j // 2, by=16)
                        load_rows(it * 2 + j // 2 + 2, j // 2)
                slot = (j - 1) % UNROLL
                if hop:
                    step_done(sp, h_row_ready, it, j, 1)
                    if hop == 1:
                        sp.dma_start(h1_rows[bass.ds((t - 1) * P, P), :], h_row[:, slot]).then_inc(h_stored[slot], 16)
                    else:
                        at = (t - 1 - TILES) * P
                        sp.dma_start(h2_rows[bass.ds(at, P), :], h_row[:, slot]).then_inc(h_stored[slot], 16)
                        sp.dma_start(h2_cols[bass.ds(at, P), :], hT[:, slot].rearrange("p k n -> p (k n)")
                                     ).then_inc(hT_stored[slot], 16)

            for j in range(UNROLL):
                if j:
                    step(0, j, 1)
                else:
                    dense(ITS, 0)
                    step_done(sp, row_landed, 0, 0, by=16)
                    load_rows(2, 0)
            with sp.Fori(1, PH - 1) as it:
                for j in range(UNROLL):
                    step(it, j, 1)
            for j in range(UNROLL):
                step(PH - 1, j, 1, False)
            for j in range(UNROLL):
                step(PH, j, 2 if j else 1, False)
            with sp.Fori(PH + 1, ITS - 2) as it:
                for j in range(UNROLL):
                    step(it, j, 2)
            for it in (ITS - 2, ITS - 1):
                for j in range(UNROLL):
                    step(it, j, 2)
            last = UNROLL - 1
            step_done(sp, h_row_ready, ITS - 1, last)
            sp.dma_start(h2_rows[E_PAD - P:E_PAD, :], h_row[:, last]).then_inc(h_stored[last], 16)
            sp.dma_start(h2_cols[E_PAD - P:E_PAD, :], hT[:, last].rearrange("p k n -> p (k n)")
                         ).then_inc(hT_stored[last], 16)

            for j in range(UNROLL):
                sp.wait_ge(h_stored[j], 16 * ITS)
                sp.wait_ge(hT_stored[j], 16 * PH)
            for jd in range(2):
                sp.wait_ge(x_turned[jd], (DENSE - jd) // 2 + 1)
                sp.wait_ge(y_summed[jd], (DENSE - jd) // 2 + 1)

            def load_h(i, slot):
                sp.dma_start(h1_in[:, slot], h1_rows[bass.ds(i * P, P), :]).then_inc(c_h_landed[slot], 16)
                sp.dma_start(h2T_in[:, slot].rearrange("p k n -> p (k n)"), h2_cols[bass.ds(i * P, P), :]
                             ).then_inc(c_h_landed[slot], 16)

            for i in range(2):
                load_h(i, i)

            def finish(it, j):
                if not isinstance(it, int) or it > ITS or j >= 2:
                    step_done(sp, c_y_summed, it - ITS, j, 2)
                load_h(it * UNROLL + (j + 2 - STEPS), (j + 2) % UNROLL)

            for j in range(UNROLL):
                finish(ITS, j)
            with sp.Fori(ITS + 1, FITS - 1) as it:
                for j in range(UNROLL):
                    finish(it, j)
            for j in range(UNROLL - 2):
                finish(FITS - 1, j)
            for j in range(UNROLL):
                sp.wait_ge(c_stored[j], 16 * PH)

        @block.gpsimd
        def _(pool):
            nc.gpsimd.memset(ident[:], 0.0)
            nc.gpsimd.memset(ones[:], 1.0).then_inc(consts_set, 1)
            nc.gpsimd.iota(counter_i[:], pattern=[[1, HI]], base=0, channel_multiplier=0).then_inc(counter_set, 1)
            pool.wait_ge(consts_set, 1)
            nc.gpsimd.affine_select(out=ident[:], in_=ident[:], compare_op=ALU.not_equal, fill=1.0,
                                    base=0, pattern=[[-1, P]], channel_multiplier=1).then_inc(consts_set, 1)
            nc.gpsimd.affine_select(out=below[:], in_=ones[:], compare_op=ALU.is_gt, fill=0.0,
                                    base=0, pattern=[[1, P]], channel_multiplier=-1).then_inc(consts_set, 1)
            pool.wait_ge(meta_cleared, 1)
            nc.gpsimd.iota(meta[:, 0:TILES, 2], pattern=[[P, TILES]], base=0,
                           channel_multiplier=1).then_inc(places_set, 1)
            limit_nodes, limit_places = (pool.to_reg(n - 1) for n in (N, E_PAD))

            def go():
                pool.sem_inc(pool_goes, 1)

            def gather(dst_ap, rows, idx, limit, landed):
                nc.gpsimd.indirect_dma_start(
                    dst_ap, None, rows[:, :], bass.IndirectOffsetOnAxis(ap=idx, axis=0),
                    bounds_check=limit, oob_is_err=False).then_inc(landed, 16)

            def scatter(rows, idx, limit, src_ap, landed):
                nc.gpsimd.indirect_dma_start(
                    rows[:, :], bass.IndirectOffsetOnAxis(ap=idx, axis=0), src_ap, None,
                    bounds_check=limit, oob_is_err=False).then_inc(landed, 16)

            def sort(it, j, rows):
                step_done(pool, rec_staged, it, j)
                go()
                scatter(rows, rec_idx[:, j:j + 1], limit_places, rec_out[:, j], rec_landed[j])

            for first, rows in ((0, by_lo), (PH, by_row)):
                with pool.Fori(first, first + PH) as it:
                    for j in range(UNROLL):
                        sort(it, j, rows)

            pool.wait_ge(table_out, 16)

            def hop1(it, j):
                step_done(pool, h_summed, it, j, UNROLL)
                step_done(pool, staged, it, j)
                go()
                gather(gath[:, j], x, a_idx[:, j, 0:1], limit_nodes, g_landed[j])
                scatter(place_of, a_idx[:, j, 1:2], limit_nodes, a_idx[:, j, 2:3], t_landed[j])

            for j in range(UNROLL):
                hop1(0, j)
            with pool.Fori(1, PH) as it:
                for j in range(UNROLL):
                    hop1(it, j)

            for j in range(UNROLL):
                pool.wait_ge(t_landed[j], 16 * PH)

            def ask(j):
                gather(q_got[:, j:j + 1], place_of, q_src[:, j:j + 1], limit_nodes, q_landed[j])

            for j in range(UNROLL):
                pool.wait_ge(q_used[j], 1)
            for j in range(UNROLL):
                ask(j)
            for j in range(UNROLL):
                pool.wait_ge(h_stored[j], 16 * PH)

            def hop2(it, j, more):
                step_done(pool, q_used, it + (1 - PH), j)
                step_done(pool, h_summed, it, j, UNROLL)
                go()
                if more:
                    ask(j)
                gather(gath[:, j], h1_rows, h_idx[:, j:j + 1], limit_places, g_landed[j])

            with pool.Fori(PH, ITS - 1) as it:
                for j in range(UNROLL):
                    hop2(it, j, True)
            for j in range(UNROLL):
                hop2(ITS - 1, j, False)

            for j in range(UNROLL):
                pool.wait_ge(h_stored[j], 16 * ITS)
            for j in range(2):
                pool.wait_ge(y_stored[j], 16 * ((DENSE - j) // 2 + 1))
            for j in range(UNROLL):
                pool.wait_ge(h_summed[j], ITS)

            def finish(it, j, behind=True, now=True):
                if now:
                    step_done(pool, h_turned, it, j, UNROLL)
                    step_done(pool, h_summed, it, j, UNROLL)
                    step_done(pool, c_staged, it - ITS, j)
                    go()
                    gather(x_dst[:, j], x, c_idx[:, j, 0:1], limit_nodes, c_x_landed[j])
                    gather(gath[:, j], h2_rows, c_idx[:, j, 2:3], limit_places, g_landed[j])
                if behind:
                    slot = (j - 3) % UNROLL
                    step_done(pool, c_ready, it - ITS, j, 3)
                    go()
                    scatter(out, o_idx[:, slot:slot + 1], limit_nodes, res[:, slot], c_stored[slot])

            for j in range(UNROLL):
                finish(ITS, j, behind=j >= 3)
            with pool.Fori(ITS + 1, FITS) as it:
                for j in range(UNROLL):
                    finish(it, j)
            for j in range(3):
                finish(FITS, j, now=False)

        @block.tensor
        def _(pe):
            pe.wait_ge(setup_done, 2)
            pe.wait_ge(consts_set, 3)

            def turn_x(dit, jd):
                n = dense_nodes(dit * 2 + jd)
                if not n:
                    return
                step_done(pe, x_landed, dit, jd, by=16)
                step_done(pe, xT_ready, dit, jd, 2)
                for r in range(2):
                    for k in range(KC):
                        last = nc.tensor.transpose(ps_x[jd][:, 2 * r + k, 0:n],
                                                   x_in[0:n, jd, r, k * P:(k + 1) * P], ident[0:n, 0:n])
                last.then_inc(x_turned[jd], 1)

            def sum_y(dit, jd):
                n = dense_nodes(dit * 2 + jd)
                if not n:
                    return
                step_done(pe, xT_ready, dit, jd)
                step_done(pe, y_ready, dit, jd, 2)
                for r in range(2):
                    for k in range(KC):
                        last = nc.tensor.matmul(ps_y[jd][0:n, r], xT[:, jd, r, k, 0:n],
                                                w_sb[:, 0, k], start=(k == 0), stop=(k == KC - 1))
                last.then_inc(y_summed[jd], 1)

            def dense(dit):
                for jd in range(2):
                    sum_y(dit, jd)
                    turn_x(dit + (jd + 1) // 2, (jd + 1) % 2)

            def wide(bank, width):
                return bank.rearrange("p k n -> p (k n)")[:, 0:width]

            def count(it, j, width, first):
                step_done(pe, hot_built, it, j)
                nc.tensor.matmul(wide(ps_h[0], width), ident_b[:], hot[:, j, 0:width],
                                 start=first and j == 0, stop=True, skip_group_check=True
                                 ).then_inc(hot_used[j], 1)

            for n, width in ((0, LO), (1, HI)):
                for j in range(UNROLL):
                    count(n * PH, j, width, True)
                with pe.Fori(n * PH + 1, (n + 1) * PH) as it:
                    for j in range(UNROLL):
                        count(it, j, width, False)
                pe.wait_ge(counts_read, n + 1)
                nc.tensor.matmul(wide(ps_h[1], width), ones[:], counts[:, 0:width], start=True, stop=True)
                nc.tensor.matmul(wide(ps_r[1], width), below[:], counts[:, 0:width],
                                 start=True, stop=True).then_inc(based, 1)
                if n == 0:
                    turn_x(0, 0)
                    dense(0)
                with pe.Fori(n * PH + (n == 0), (n + 1) * PH) as it:
                    dense(it)

            pe.wait_ge(cols_f, 2)
            pe.wait_ge(upto_set, 6)
            for half in range(2):
                for n, a in enumerate((col_r, tidx_r, row_r, val_r)):
                    last = nc.tensor.transpose(ps_r[half][:, n, 0:EROWS], a[:, half * P:(half + 1) * P],
                                               ident[0:EROWS, 0:EROWS])
            last.then_inc(meta_turned, 1)
            pe.wait_ge(meta_ready, 1)

            def turn_h(it, j):
                b = (j - 1) % 2
                step_done(pe, hT_ready, it, j, 1)
                step_done(pe, h_row_ready, it, j, 3)
                for k in range(KC):
                    last = nc.tensor.transpose(ps_r[b][:, k], hT[:, (j - 1) % UNROLL, k], ident[:])
                last.then_inc(h_turned[(j - 1) % UNROLL], 1)

            def sum_h(it, j):
                step_done(pe, g_landed, it, j, by=16)
                step_done(pe, s_built, it, j)
                step_done(pe, hT_ready, it, j, 2)
                for k in range(KC):
                    last = nc.tensor.matmul(ps_h[j % 2][:, k], gath[:, j, k * P:(k + 1) * P], S[:, j],
                                            start=True, stop=True)
                last.then_inc(h_summed[j], 1)

            def step(it, j, behind=True):
                dit, jd = it + ITS, j // 2
                if j % 2 == 0:
                    sum_y(dit, jd)
                else:
                    turn_x(dit + (jd + 1) // 2, (jd + 1) % 2)
                if behind:
                    turn_h(it, j)
                sum_h(it, j)

            for j in range(UNROLL):
                step(0, j, j > 0)
            with pe.Fori(1, ITS - 2) as it:
                for j in range(UNROLL):
                    step(it, j)
            for it in (ITS - 2, ITS - 1):
                for j in range(UNROLL):
                    step(it, j)
            turn_h(ITS, 0)

            step_done(pe, xT_ready, DITS - 1, 0)
            step_done(pe, y_ready, DITS - 1, 0)
            step_done(pe, y_ready, DITS - 2, 1)
            for j in (UNROLL - 2, UNROLL - 1):
                step_done(pe, h_row_ready, ITS - 1, j)

            def turn_all(it, j):
                step_done(pe, c_x_landed, it - ITS, j, by=16)
                step_done(pe, c_h_landed, it - ITS, j, by=2 * 16)
                step_done(pe, h_row_ready, it, j, 2)
                for k in range(KC):
                    cols = slice(k * P, (k + 1) * P)
                    nc.tensor.transpose(ps_x[j % 2][:, k], x_dst[:, j, cols], ident[:])
                    last = nc.tensor.transpose(ps_x[j % 2][:, KC + k], h1_in[:, j, cols], ident[:])
                last.then_inc(h_turned[j], 1)

            def sum_all(it, j):
                b, slot = (j - 1) % 2, (j - 1) % UNROLL
                step_done(pe, h_row_ready, it, j, 1)
                step_done(pe, hT_ready, it, j, 1)
                step_done(pe, c_ready, it - ITS, j, 3)
                operands = ([cT[:, slot, n] for n in range(2 * KC)] + [h2T_in[:, slot, k] for k in range(KC)]
                            + [hT[:, slot, k] for k in range(KC)])
                for n, lhsT in enumerate(operands):
                    last = nc.tensor.matmul(ps_y[b][:, 0], lhsT, w_sb[:, n // KC, n % KC],
                                            start=(n == 0), stop=(n == len(operands) - 1))
                last.then_inc(c_y_summed[slot], 1)

            def finish(it, j, behind=True):
                turn_all(it, j)
                sum_h(it, j)
                if behind:
                    sum_all(it, j)

            for j in range(UNROLL):
                finish(ITS, j, j > 0)
            with pe.Fori(ITS + 1, FITS) as it:
                for j in range(UNROLL):
                    finish(it, j)
            sum_all(FITS, 0)

        @block.scalar
        def _(act):
            def put_xT(dit, jd):
                n = dense_nodes(dit * 2 + jd)
                if not n:
                    return
                step_done(act, x_turned, dit, jd)
                step_done(act, y_summed, dit, jd, 2)
                nc.scalar.activation(xT[:, jd].rearrange("p r k n -> p (r k) n")[:, :, 0:n],
                                     ps_x[jd][:, :, 0:n], ACT.Copy).then_inc(xT_ready[jd], 1)

            def deviation(dit, jd):
                n = dense_nodes(dit * 2 + jd)
                if n:
                    step_done(act, mv_ready, dit, jd)
                    nc.scalar.activation(std[0:n, jd], mv[0:n, jd, :, 1], ACT.Sqrt, bias=eps[0:n]
                                         ).then_inc(std_ready[jd], 1)

            def norm(dit, jd):
                n = dense_nodes(dit * 2 + jd)
                if not n:
                    return
                step_done(act, nmr_ready, dit, jd)
                step_done(act, y_stored, dit, jd, 2, by=16)
                for r in range(2):
                    last = nc.scalar.activation(y_out[0:n, jd, r], ps_y[jd][0:n, r], ACT.Identity,
                                                bias=nmr[0:n, jd, r:r + 1], scale=rstd[0:n, jd, r:r + 1])
                last.then_inc(y_ready[jd], 1)

            def dense(dit):
                for jd in range(2):
                    put_xT(dit + (jd + 1) // 2, (jd + 1) % 2)
                    deviation(dit, jd)
                    norm(dit, jd)

            act.wait_ge(setup_done, 2)
            put_xT(0, 0)
            dense(0)
            with act.Fori(1, ITS) as it:
                dense(it)

            def put_h_row(it, j):
                slot = (j - 1) % UNROLL
                step_done(act, h_turned, it, j, 1)
                step_done(act, h_stored, it, j, 1 + UNROLL, by=16)
                nc.scalar.activation(h_row[:, slot], ps_r[(j - 1) % 2][:, 0:KC].rearrange("p k n -> p (k n)"),
                                     ACT.Copy).then_inc(h_row_ready[slot], 1)

            def step(it, j, behind=True):
                dit, jd = it + ITS, j // 2
                if j % 2 == 0:
                    if behind:
                        put_h_row(it, j)
                    deviation(dit, jd)
                else:
                    put_xT(dit + (jd + 1) // 2, (jd + 1) % 2)
                    put_h_row(it, j)
                    norm(dit, jd)

            for j in range(UNROLL):
                step(0, j, j > 0)
            with act.Fori(1, ITS - 2) as it:
                for j in range(UNROLL):
                    step(it, j)
            for it in (ITS - 2, ITS - 1):
                for j in range(UNROLL):
                    step(it, j)
            put_h_row(ITS, 0)

            def put_cT(it, j):
                step_done(act, h_turned, it, j)
                step_done(act, c_y_summed, it - ITS, j, UNROLL)
                nc.scalar.activation(cT[:, j], ps_x[j % 2][:], ACT.Copy).then_inc(h_row_ready[j], 1)

            def c_norm(it, j):
                b, slot = (j - 1) % 2, (j - 1) % UNROLL
                step_done(act, c_mv_ready, it - ITS, j, 1)
                nc.scalar.activation(std[:, b, 0:1], mv[:, b, 0, 1:2], ACT.Sqrt, bias=eps[:]
                                     ).then_inc(c_std_ready[slot], 1)
                step_done(act, c_nmr_ready, it - ITS, j, 1)
                step_done(act, c_stored, it - ITS, j, 1 + UNROLL, by=16)
                nc.scalar.activation(res[:, slot], ps_y[b][:, 0], ACT.Identity, bias=nmr[:, b, 0:1],
                                     scale=rstd[:, b, 0:1]).then_inc(c_ready[slot], 1)

            for jd in range(2):
                act.wait_ge(y_stored[jd], 16 * ((DENSE - jd) // 2 + 1))
            for j in range(UNROLL):
                put_cT(ITS, j)
                if j:
                    c_norm(ITS, j)
            with act.Fori(ITS + 1, FITS) as it:
                for j in range(UNROLL):
                    put_cT(it, j)
                    c_norm(it, j)
            c_norm(FITS, 0)

        @block.vector
        def _(dve):
            nc.vector.memset(row_in[:], PAD_ROW)
            nc.vector.memset(col_in[:], 0)
            nc.vector.memset(val_in[:], 0.0)
            nc.vector.memset(nowhere[:], NOWHERE).then_inc(pads_set, 1)
            nc.vector.memset(eps[:], EPS)
            nc.vector.memset(ones_w[:], 1.0)
            nc.vector.memset(row_b[:, 0:1], -2.0)
            nc.vector.memset(rec[:], 0)
            nc.vector.memset(next_r[:], PAD_ROW)
            nc.vector.memset(meta[:], 0).then_inc(meta_cleared, 1)
            dve.wait_ge(counter_set, 1)
            nc.vector.tensor_copy(counter[:], counter_i[:])
            nc.vector.tensor_copy(counter_h[:], counter_i[:]).then_inc(counter_set, 1)
            dve.wait_ge(edges_in, 6 * 16)
            dve.wait_ge(meta_cleared, 1)
            nc.vector.tensor_copy(rec[:, :, 0], row_in[:])
            nc.vector.tensor_copy(rec[:, :, 1], col_in[:])
            nc.vector.tensor_copy(rec[:, :, 2].bitcast(F32), val_in[:]).then_inc(digits_set, 1)
            dve.wait_ge(consts_set, 2)
            nc.vector.tensor_copy(ident_b[:], ident[:])
            dve.wait_ge(w_in, 16)
            nc.vector.tensor_copy(w_sb[:].rearrange("p h k o -> p k o h"),
                                  w_raw[:].rearrange("p k (o h) -> p k o h", h=HOPS + 1)).then_inc(setup_done, 1)
            dve.wait_ge(setup_done, 1)
            for k in range(KC):
                block_k = w_sb[:, 0, k, k * P:(k + 1) * P]
                last = nc.vector.tensor_tensor(block_k, block_k, ident[:], ALU.add)
            last.then_inc(setup_done, 1)
            dve.wait_ge(counter_set, 2)
            dve.wait_ge(digits_set, 1)

            def digits(n):
                if n == 0:
                    nc.vector.tensor_scalar(digit_i[:], rec[:, :, 0], LO - 1, None, ALU.bitwise_and
                                            ).then_inc(digits_set, 1)
                else:
                    nc.vector.tensor_scalar(digit_i[:], rec[:, :, 0], LO.bit_length() - 1, None,
                                            ALU.logical_shift_right).then_inc(digits_set, 1)
                dve.wait_ge(digits_set, 2 * n + 2)
                nc.vector.tensor_copy(digit[:], digit_i[:]).then_inc(digits_set, 1)
                dve.wait_ge(digits_set, 2 * n + 3)

            def one_hot(it, n, j, width):
                step_done(dve, hot_used, it, j, UNROLL)
                nc.vector.tensor_scalar(hot[:, j, 0:width], counter_h[:, 0:width],
                                        digit[:, bass.ds(it * UNROLL + (j - n * TILES), 1)], None,
                                        ALU.is_equal).then_inc(hot_built[j], 1)

            def first_places(n, width):
                for j in range(UNROLL):
                    dve.wait_ge(hot_used[j], (n + 1) * PH)
                nc.vector.tensor_copy(counts[:, 0:width], ps_h[0].rearrange("p k n -> p (k n)")[:, 0:width]
                                      ).then_inc(counts_read, 1)
                dve.wait_ge(based, n + 1)
                total = ps_h[1].rearrange("p k n -> p (k n)")[:, 0:width]
                lower = ps_r[1].rearrange("p k n -> p (k n)")[:, 0:width]
                nc.vector.tensor_tensor_scan(upto[:, 0:width], ones_w[:, 0:width], total, 0.0,
                                             ALU.mult, ALU.add).then_inc(upto_set, 1)
                dve.wait_ge(upto_set, 3 * n + 1)
                nc.vector.tensor_tensor(upto[:, 0:width], upto[:, 0:width], total, ALU.subtract).then_inc(upto_set, 1)
                dve.wait_ge(upto_set, 3 * n + 2)
                nc.vector.tensor_tensor(place[:, 0:width], upto[:, 0:width], lower, ALU.add).then_inc(upto_set, 1)
                dve.wait_ge(upto_set, 3 * n + 3)

            def sort(it, n, j, width):
                t = it * UNROLL + (j - n * TILES)
                d_t = digit[:, bass.ds(t, 1)]
                step_done(dve, rec_landed, it, j, UNROLL, by=16)
                step_done(dve, place_moved, it, j, 1)
                nc.vector.scalar_tensor_tensor(picked[:, 0:width], counter[:, 0:width], d_t, place[:, 0:width],
                                               ALU.is_equal, ALU.mult, accum_out=place_f[:, j:j + 1])
                nc.vector.scalar_tensor_tensor(place[:, 0:width], counter[:, 0:width], d_t, place[:, 0:width],
                                               ALU.is_equal, ALU.add).then_inc(place_moved[j], 1)
                nc.vector.tensor_scalar(rec_out[:, j], rec[:, bass.ds(t, 1)].rearrange("p o w -> p (o w)"),
                                        0, None, ALU.bitwise_or)

            def hand_over(it, j):
                step_done(dve, place_moved, it, j)
                nc.vector.tensor_copy(rec_idx[:, j:j + 1], place_f[:, j:j + 1]).then_inc(rec_staged[j], 1)

            def measure(dit, jd):
                n = dense_nodes(dit * 2 + jd)
                if not n:
                    return
                step_done(dve, y_summed, dit, jd)
                for r in range(2):
                    last = nc.vector.bn_stats(stats[0:n, jd, r], ps_y[jd][0:n, r])
                last.then_inc(stats_ready[jd], 1)
                step_done(dve, stats_ready, dit, jd)

            def mean_variance(dit, jd):
                n = dense_nodes(dit * 2 + jd)
                if not n:
                    return
                for r in range(2):
                    last = nc.vector.bn_aggr(mv[0:n, jd, r], stats[0:n, jd, r])
                last.then_inc(mv_ready[jd], 1)

            def factors(dit, jd):
                n = dense_nodes(dit * 2 + jd)
                if not n:
                    return
                step_done(dve, std_ready, dit, jd)
                nc.vector.reciprocal(rstd[0:n, jd], std[0:n, jd]).then_inc(rstd_ready[jd], 1)
                step_done(dve, rstd_ready, dit, jd)
                nc.vector.scalar_tensor_tensor(nmr[0:n, jd], mv[0:n, jd, :, 0], -1.0, rstd[0:n, jd],
                                               ALU.mult, ALU.mult).then_inc(nmr_ready[jd], 1)

            def sort_four(it, n, width):
                for j in range(UNROLL):
                    sort(it, n, j, width)
                    if j % 2 == 0:
                        measure(it, j // 2)
                    hand_over(it, j)
                    if j % 2 == 0:
                        mean_variance(it, j // 2)
                    else:
                        factors(it, j // 2)

            for n, width in ((0, LO), (1, HI)):
                if n:
                    dve.wait_ge(records_in, 16)
                digits(n)
                if n == 0:
                    for j in range(UNROLL):
                        one_hot(0, n, j, width)
                with dve.Fori(n * PH + (n == 0), (n + 1) * PH) as it:
                    for j in range(UNROLL):
                        one_hot(it, n, j, width)
                first_places(n, width)
                if n == 0:
                    sort_four(0, n, width)
                with dve.Fori(n * PH + (n == 0), (n + 1) * PH) as it:
                    sort_four(it, n, width)

            nc.vector.memset(hT[:], 0.0)
            nc.vector.memset(x_dst[:], 0.0).then_inc(meta_cleared, 1)
            dve.wait_ge(records_in, 4 * 16)
            nc.vector.tensor_copy(row_r[:], rec_r[:, :, 0]).then_inc(cols_f, 1)
            nc.vector.tensor_copy(col_r[:], rec_r[:, :, 1])
            nc.vector.tensor_copy(val_r[:], rec_r[:, :, 2].bitcast(F32))
            nc.vector.tensor_tensor(last_r[:], rec_r[:, :, 0], next_r[:, :, 0], ALU.not_equal).then_inc(shifted, 1)
            dve.wait_ge(shifted, 1)
            nc.vector.scalar_tensor_tensor(tidx_r[:], row_r[:], float(-NOWHERE), last_r[:],
                                           ALU.add, ALU.mult).then_inc(shifted, 1)
            dve.wait_ge(shifted, 2)
            nc.vector.tensor_scalar(tidx_r[:], tidx_r[:], float(NOWHERE), None, ALU.add).then_inc(cols_f, 1)
            dve.wait_ge(meta_turned, 1)
            dve.wait_ge(places_set, 1)
            dve.wait_ge(meta_cleared, 2)
            for half in range(2):
                tiles = slice(half, TILES, 2)
                nc.vector.tensor_copy(meta[:, tiles, 0], ps_r[half][:, 0, 0:EROWS])
                nc.vector.tensor_copy(meta[:, tiles, 1], ps_r[half][:, 1, 0:EROWS])
                nc.vector.tensor_copy(r_col[:, tiles], ps_r[half][:, 2, 0:EROWS])
                last = nc.vector.tensor_copy(v_col[:, tiles], ps_r[half][:, 3, 0:EROWS])
            last.then_inc(meta_ready, 1)
            dve.wait_ge(meta_ready, 1)

            def stage(it, j):
                step_done(dve, g_landed, it, j, UNROLL, by=16)
                step_done(dve, t_landed, it, j, UNROLL, by=16)
                nc.vector.tensor_copy(a_idx[:, j], meta[:, bass.ds(it * UNROLL + j, 1), 0:3].rearrange(
                    "p o n -> p (o n)")).then_inc(staged[j], 1)

            def ask_later(i, j):
                nc.vector.tensor_copy(q_src[:, j:j + 1], meta[:, bass.ds(i, 1), 0]).then_inc(q_used[j], 1)

            def use_place(it, j):
                i = it * UNROLL + (j - TILES)
                step_done(dve, q_landed, it - PH, j, by=16)
                nc.vector.scalar_tensor_tensor(v_col[:, bass.ds(i + TILES, 1)], q_got[:, j:j + 1], float(E_PAD),
                                               v_col[:, bass.ds(i, 1)], ALU.is_lt, ALU.mult)
                nc.vector.tensor_copy(h_idx[:, j:j + 1], q_got[:, j:j + 1])
                nc.vector.tensor_copy(meta[:, bass.ds(i, 1), 3], q_got[:, j:j + 1])
                ask_later(i + UNROLL, j)

            def build(it, j, hop):
                i = it * UNROLL + (j - (hop - 1) * TILES)
                if hop == 1:
                    step_done(dve, row_landed, it, j // 2, by=16)
                if hop == 2:
                    step_done(dve, q_used, it - PH + 1, j)
                nc.vector.tensor_scalar(S[:, j], row_b[:, bass.ds(i * P + 1, P)], r_col[:, bass.ds(i, 1)],
                                        v_col[:, bass.ds(i + (TILES if hop > 1 else 0), 1)],
                                        ALU.is_equal, ALU.mult)
                nc.vector.tensor_scalar(same[:, j], row_b[:, bass.ds(i * P + 1, P)], row_b[:, bass.ds(i * P, 1)],
                                        None, ALU.is_equal).then_inc(s_built[j], 1)

            def carry(it, j):
                step_done(dve, h_summed, it, j)
                step_done(dve, s_built, it, j)
                step_done(dve, hT_ready, it, j, 1)
                for k in range(KC):
                    last = nc.vector.scalar_tensor_tensor(
                        hT[:, j, k], same[:, j], hT[:, (j - 1) % UNROLL, k, P - 1:P], ps_h[j % 2][:, k],
                        ALU.mult, ALU.add)
                last.then_inc(hT_ready[j], 1)

            def next_of(it, j, ahead):
                return it + (j + ahead) // UNROLL, (j + ahead) % UNROLL

            def step(it, j, hop, stages=True, builds=True):
                dit, jd = it + ITS, j // 2
                if hop == 1:
                    stage(*next_of(it, j, 3))
                    if builds:
                        build(*next_of(it, j, 1), 1)
                else:
                    if stages:
                        use_place(*next_of(it, j, 3))
                    if builds:
                        build(*next_of(it, j, 1), 2)
                if j % 2 == 0:
                    measure(dit, jd)
                step_done(dve, h_turned, it, j, UNROLL)
                if hop == 2 and not (isinstance(it, int) and it == PH):
                    step_done(dve, hT_stored, it - PH, j, UNROLL, by=16)
                carry(it, j)
                if j % 2 == 0:
                    mean_variance(dit, jd)
                else:
                    factors(dit, jd)

            for j in range(UNROLL - 1):
                stage(0, j)
            build(0, 0, 1)
            for j in range(UNROLL):
                step(0, j, 1)
            with dve.Fori(1, PH - 1) as it:
                for j in range(UNROLL):
                    step(it, j, 1)
            for j in range(UNROLL):
                step(PH - 1, j, 1, builds=j < UNROLL - 1)
            for j in range(UNROLL):
                ask_later(j, j)
            for j in range(UNROLL - 1):
                use_place(PH, j)
            build(PH, 0, 2)
            for j in range(UNROLL):
                step(PH, j, 2)
            with dve.Fori(PH + 1, ITS - 1) as it:
                for j in range(UNROLL):
                    step(it, j, 2)
            for j in range(UNROLL):
                step(ITS - 1, j, 2, j == 0, j < UNROLL - 1)

            def c_stage(it, j):
                step_done(dve, c_x_landed, it - ITS, j, UNROLL, by=16)
                step_done(dve, g_landed, it, j, UNROLL, by=16)
                nc.vector.tensor_copy(c_idx[:, j], meta[:, bass.ds(it * UNROLL + (j - STEPS), 1), 1:4].rearrange(
                    "p o n -> p (o n)")).then_inc(c_staged[j], 1)

            def c_measure(it, j):
                b, slot = (j - 1) % 2, (j - 1) % UNROLL
                step_done(dve, c_y_summed, it - ITS, j, 1)
                nc.vector.bn_stats(stats[:, b, 0], ps_y[b][:, 0]).then_inc(c_stats_ready[slot], 1)
                step_done(dve, c_stored, it - ITS, j, 1 + UNROLL, by=16)
                step_done(dve, c_stats_ready, it - ITS, j, 1)
                nc.vector.tensor_copy(o_idx[:, slot:slot + 1], meta[:, bass.ds(it * UNROLL + (j - 1 - STEPS), 1), 1])
                nc.vector.bn_aggr(mv[:, b, 0], stats[:, b, 0]).then_inc(c_mv_ready[slot], 1)

            def c_factors(it, j):
                b, slot = (j - 1) % 2, (j - 1) % UNROLL
                step_done(dve, c_std_ready, it - ITS, j, 1)
                nc.vector.reciprocal(rstd[:, b, 0:1], std[:, b, 0:1]).then_inc(c_rstd_ready[slot], 1)
                step_done(dve, c_rstd_ready, it - ITS, j, 1)
                nc.vector.scalar_tensor_tensor(nmr[:, b, 0:1], mv[:, b, 0, 0:1], -1.0, rstd[:, b, 0:1],
                                               ALU.mult, ALU.mult).then_inc(c_nmr_ready[slot], 1)

            def finish(it, j, behind=True, builds=True):
                c_stage(*next_of(it, j, 3))
                if builds:
                    build(*next_of(it, j, 1), 3)
                step_done(dve, c_y_summed, it - ITS, j, UNROLL)
                carry(it, j)
                if behind:
                    c_measure(it, j)
                    c_factors(it, j)

            for j in range(UNROLL):
                dve.wait_ge(q_used[j], PH + 1)
                dve.wait_ge(hT_stored[j], 16 * PH)
            for j in range(UNROLL - 1):
                c_stage(ITS, j)
            build(ITS, 0, 3)
            for j in range(UNROLL):
                finish(ITS, j, j > 0)
            with dve.Fori(ITS + 1, FITS - 1) as it:
                for j in range(UNROLL):
                    finish(it, j)
            for j in range(UNROLL):
                finish(FITS - 1, j, builds=j < UNROLL - 1)
            c_measure(FITS, 0)
            c_factors(FITS, 0)


_INS = ['x', 'src', 'dst', 'edge_weight', 'L0_gnn_weight']


def kernel(**inputs):
    import numpy as _np
    import concourse.bacc as _bacc
    from concourse import mybir as _mybir
    from concourse.bass_utils import run_bass_kernel_spmd as _run

    nc = _bacc.Bacc("TRN2", target_bir_lowering=False, num_devices=1)
    arrays, args = {}, []
    for name in _INS:
        a = _np.ascontiguousarray(inputs[name])
        arrays[f"in_{name}_dram"] = a
        args.append(nc.dram_tensor(f"in_{name}_dram", a.shape, _mybir.dt.from_np(a.dtype), kind="ExternalInput").ap())
    shape = inputs['x'].shape
    args.append(nc.dram_tensor("out_0_dram", shape, _mybir.dt.float32, kind="ExternalOutput").ap())
    gnn_program(nc, *args)
    r = _run(nc, [arrays], core_ids=[0])
    return r.results[0]["out_0_dram"]
```

```python
from contextlib import ExitStack

import concourse.bass as bass
from concourse import mybir

P = 128
F32 = mybir.dt.float32
F16 = mybir.dt.float16
BF16 = mybir.dt.bfloat16
I32 = mybir.dt.int32
ALU = mybir.AluOpType
ACT = mybir.ActivationFunctionType

EPS = 1e-5
UNROLL = 4
NOWHERE = 1 << 20


def step_done(eng, sems, it, j, back=0, by=1):
    times = it + (j - back) // len(sems) + 1
    if isinstance(times, int) and times <= 0:
        return
    eng.wait_ge(sems[(j - back) % len(sems)], times * by)


def iterations(eng, first, end, body):
    if (end - first) % 2:
        body(first)
        first += 1
    with eng.Fori(0, (end - first) // 2) as r:
        for u in range(2):
            body(r * 2 + (first + u))


def gnn_program(nc, x, row, col, value, weight, out):
    N, C = x.shape
    E = row.shape[0]
    CO = weight.shape[1]
    HOPS = weight.shape[2] - 1
    KC = C // P
    TILES = -(-E // (P * UNROLL)) * UNROLL
    E_PAD = TILES * P
    STEPS = 2 * TILES
    ITS = STEPS // UNROLL
    PH = TILES // UNROLL
    ROWS = 2 * P
    DENSE = N // ROWS
    TAIL = N - DENSE * ROWS
    TAIL_P = TAIL // 2
    META = TILES + UNROLL
    NT = -(-N // P)
    EROWS = TILES // 2
    LO = 256
    HI = N // LO + 2
    PAD_ROW = (HI - 1) * LO
    REC = 4
    FITS = ITS + PH
    KITS = (PH - 1) // 2
    SDITS = 2 * (KITS + PH) + 1
    DITS = SDITS + PH
    assert C == 2 * P and CO == 2 * P and HOPS == 3 and TILES % UNROLL == 0
    assert PH % 2 == 1 and DENSE == 2 * (DITS - 1) and TAIL % 2 == 0 and 0 < TAIL_P <= P
    assert N <= PAD_ROW < NOWHERE and LO <= 512 and HI <= 512

    h1_rows = nc.dram_tensor("h1_rows", (E_PAD, C), F32, kind="Internal").ap()
    h2_rows = nc.dram_tensor("h2_rows", (E_PAD, C), F32, kind="Internal").ap()
    place_of = nc.dram_tensor("place_of", (NT * P, 1), I32, kind="Internal").ap()
    side = nc.dram_tensor("side", (E_PAD, C + CO), F32, kind="Internal").ap()
    by_lo = nc.dram_tensor("by_lo", (E_PAD, REC), I32, kind="Internal").ap()
    by_row = nc.dram_tensor("by_row", (E_PAD, REC), I32, kind="Internal").ap()
    row_line = nc.dram_tensor("row_line", (E_PAD,), F32, kind="Internal").ap()

    with ExitStack() as ctx:
        def sb(name, shape, dt=F32):
            return ctx.enter_context(nc.sbuf_tensor(name, shape, dt))

        def sem(name):
            return ctx.enter_context(nc.semaphore(name))

        def sems(name, n=UNROLL):
            return [sem(f"{name}{i}") for i in range(n)]

        ident = sb("ident", [P, P])
        w_sb = sb("w_sb", [P, HOPS + 1, KC, CO])
        eps = sb("eps", [P, 1])
        ident_b = sb("ident_b", [P, P], BF16)
        ones = sb("ones", [P, P])
        below = sb("below", [P, P])
        row_b = sb("row_b", [P, 1 + E_PAD])
        taken = [1 + E_PAD]

        def early(shape, dt=F32):
            each = 4 // mybir.dt.size(dt)
            n = shape[1] * (shape[2] if len(shape) > 2 else 1)
            taken[0] -= -(-n // each)
            a = row_b[0:shape[0], taken[0]:taken[0] + -(-n // each)]
            if dt != F32:
                a = a.bitcast(dt)
            return a.rearrange("p (a b) -> p a b", b=shape[2]) if len(shape) > 2 else a

        counter_i = early([P, HI], I32)
        counter = early([P, HI])
        counter_h = early([P, HI], F16)
        row_in = early([P, TILES], I32)
        col_in = early([P, TILES], I32)
        val_in = early([P, TILES])
        rec = early([P, TILES, REC], I32)
        digit_i = early([P, TILES], I32)
        digit = early([P, 2 * TILES])
        hot = early([P, 2 * UNROLL, HI], BF16)
        counts = early([P, HI])
        upto = early([P, HI])
        ones_w = early([P, HI])
        place = early([P, HI])
        picked = early([P, UNROLL, HI])
        matched = early([P, 2 * UNROLL, TILES])
        rank = early([P, TILES])
        rec_r = early([EROWS, 2 * P, REC], I32)
        next_r = early([EROWS, 2 * P, REC], I32)
        val_r = early([EROWS, 2 * P])
        col_r = early([EROWS, 2 * P])
        row_r = early([EROWS, 2 * P])
        last_r = early([EROWS, 2 * P])
        tidx_r = early([EROWS, 2 * P])
        nowhere = early([P, NT], I32)
        w_raw = early([P, KC, CO * (HOPS + 1)])
        place_f = sb("place_f", [P, UNROLL])
        rec_idx = sb("rec_idx", [P, UNROLL], I32)
        rec_out = sb("rec_out", [P, UNROLL, REC], I32)
        meta = sb("meta", [P, META, 4], I32)
        r_col = sb("r_col", [P, TILES])
        v_col = sb("v_col", [P, STEPS])
        a_idx = sb("a_idx", [P, UNROLL, 3], I32)
        q_src = sb("q_src", [P, UNROLL], I32)
        q_got = sb("q_got", [P, UNROLL], I32)
        h_idx = sb("h_idx", [P, UNROLL], I32)
        c_idx = sb("c_idx", [P, UNROLL, 3], I32)
        o_idx = sb("o_idx", [P, UNROLL], I32)
        gath = sb("gath", [P, UNROLL, C])
        S = sb("S", [P, UNROLL, P])
        same = sb("same", [P, UNROLL, P])
        hT = sb("hT", [P, UNROLL, KC, P])
        h_row = sb("h_row", [P, UNROLL, C])
        wait_pad = sb("wait_pad", [P, 1])
        x_in = sb("x_in", [P, 2, 2, C])
        xT = sb("xT", [P, 2, 2, KC, P])
        stats = sb("stats", [P, 2, 2, 6])
        mv = sb("mv", [P, 2, 2, 2])
        std = sb("std", [P, 2, 2])
        rstd = sb("rstd", [P, 2, 2])
        nmr = sb("nmr", [P, 2, 2])
        y_out = sb("y_out", [P, 2, 2, CO])
        h1T = sb("h1T", [P, UNROLL, P])
        p_out = sb("p_out", [P, UNROLL, CO])
        x_dst = sb("x_dst", [P, UNROLL, C])
        cT = sb("cT", [P, UNROLL, KC, P])
        side_in = sb("side_in", [P, UNROLL, P + CO])
        y_sum = sb("y_sum", [P, UNROLL, CO])
        res = y_out[:].rearrange("p d r c -> p (d r) c")

        ps_x = [ctx.enter_context(nc.psum_tensor(f"ps_x{i}", [P, 4, P], F32)) for i in range(2)]
        ps_y = [ctx.enter_context(nc.psum_tensor(f"ps_y{i}", [P, 2, CO], F32)) for i in range(2)]
        ps_h = [ctx.enter_context(nc.psum_tensor(f"ps_h{i}", [P, 4, P], F32)) for i in range(2)]
        ps_r = [ctx.enter_context(nc.psum_tensor(f"ps_r{i}", [P, 4, P], F32)) for i in range(2)]

        pads_set = sem("pads_set")
        edges_in = sem("edges_in")
        w_in = sem("w_in")
        consts_set = sem("consts_set")
        counter_set = sem("counter_set")
        digits_set = sem("digits_set")
        hot_built = sems("hot_built", 2)
        hot_used = sems("hot_used", 2)
        counts_read = sem("counts_read")
        based = sem("based")
        upto_set = sem("upto_set")
        places_picked = sems("places_picked", 2)
        rec_staged = sems("rec_staged", 2)
        rec_landed = sems("rec_landed")
        records_in = sem("records_in")
        cols_f = sem("cols_f")
        line_out = sem("line_out")
        table_out = sem("table_out")
        shifted = sem("shifted")
        meta_turned = sem("meta_turned")
        meta_cleared = sem("meta_cleared")
        places_set = sem("places_set")
        setup_done = sem("setup_done")
        meta_ready = sem("meta_ready")
        pool_goes = sem("pool_goes")
        x_landed = sems("x_landed", 2)
        y_stored = sems("y_stored", 2)
        row_landed = sems("row_landed", 2)
        g_landed = sems("g_landed")
        t_landed = sems("t_landed")
        q_landed = sems("q_landed")
        h_stored = sems("h_stored")
        hT_stored = sems("hT_stored")
        side_landed = sems("side_landed")
        p_stored = sems("p_stored")
        x_turned = sems("x_turned", 2)
        xT_ready = sems("xT_ready", 2)
        y_summed = sems("y_summed", 2)
        stats_ready = sems("stats_ready", 2)
        mv_ready = sems("mv_ready", 2)
        std_ready = sems("std_ready", 2)
        rstd_ready = sems("rstd_ready", 2)
        nmr_ready = sems("nmr_ready", 2)
        y_ready = sems("y_ready", 2)
        staged = sems("staged")
        q_used = sems("q_used")
        s_built = sems("s_built")
        h_summed = sems("h_summed")
        hT_ready = sems("hT_ready")
        h_turned = sems("h_turned")
        h_row_ready = sems("h_row_ready")
        p_summed = sems("p_summed")
        p_ready = sems("p_ready")
        c_x_landed = sems("c_x_landed")
        c_stored = sems("c_stored")
        c_staged = sems("c_staged")
        c_y_summed = sems("c_y_summed")
        c_ready = sems("c_ready")
        c_added = sems("c_added", 2)
        c_stats_ready = sems("c_stats_ready", 2)
        c_mv_ready = sems("c_mv_ready", 2)
        c_std_ready = sems("c_std_ready", 2)
        c_rstd_ready = sems("c_rstd_ready", 2)
        c_nmr_ready = sems("c_nmr_ready", 2)

        def dense_nodes(d):
            return P if not isinstance(d, int) or d < DENSE else TAIL_P if d == DENSE else 0

        def dense_rows(a, t):
            return a[bass.ds(t * ROWS, ROWS), :].rearrange("(p r) c -> p r c", r=2)

        def tail_of(a):
            return a[DENSE * ROWS:N, :].rearrange("(p r) c -> p r c", r=2)

        block = ctx.enter_context(nc.Block())

        @block.sync
        def _(sp):
            for d in range(2):
                sp.dma_start(x_in[:, d], dense_rows(x, d)).then_inc(x_landed[d], 16)
            sp.wait_ge(pads_set, 1)
            full = E // TILES
            for tile, a in ((row_in, row), (col_in, col), (val_in, value)):
                sp.dma_start(tile[0:full, :], a[0:full * TILES].rearrange("(p t) -> p t", t=TILES)
                             ).then_inc(edges_in, 16)
                sp.dma_start(tile[full:full + 1, 0:E - full * TILES],
                             a[full * TILES:E].rearrange("(o n) -> o n", o=1)).then_inc(edges_in, 16)
            sp.dma_start(w_raw[:], weight.rearrange("(k p) o h -> p k (o h)", p=P)).then_inc(w_in, 16)
            sp.dma_start(place_of.rearrange("(p t) o -> p (t o)", p=P), nowhere[:]).then_inc(table_out, 16)

            def dense(dit, jd):
                d = dit * 2 + jd
                fixed = isinstance(d, int)
                slot = (jd + 1) % 2
                if not fixed or d + 3 <= DENSE:
                    step_done(sp, x_turned, dit, jd, -1)
                    if fixed and d + 3 == DENSE:
                        sp.dma_start(x_in[0:TAIL_P, slot], tail_of(x)).then_inc(x_landed[slot], 16)
                    else:
                        sp.dma_start(x_in[:, slot], dense_rows(x, d + 3)).then_inc(x_landed[slot], 16)
                if not fixed or d > 0:
                    step_done(sp, y_ready, dit, jd, 1)
                    if fixed and d - 1 == DENSE:
                        sp.dma_start(tail_of(out), y_out[0:TAIL_P, slot]).then_inc(y_stored[slot], 16)
                    else:
                        sp.dma_start(dense_rows(out, d - 1), y_out[:, slot]).then_inc(y_stored[slot], 16)

            step_done(sp, x_turned, 0, 0)
            sp.dma_start(x_in[:, 0], dense_rows(x, 2)).then_inc(x_landed[0], 16)
            dense(0, 0)
            dense(0, 1)
            def dense_pair(dit):
                dense(dit, 0)
                dense(dit, 1)

            iterations(sp, 1, KITS + PH, dense_pair)
            dense(KITS + PH, 0)
            for j in range(UNROLL):
                sp.wait_ge(rec_landed[j], 16 * PH)
            sp.dma_start(rec[:], by_lo.rearrange("(p t) w -> p t w", t=TILES)).then_inc(records_in, 16)
            dense(KITS + PH, 1)
            iterations(sp, KITS + PH + 1, SDITS - 1, dense_pair)
            dense(SDITS - 1, 0)
            for j in range(UNROLL):
                sp.wait_ge(rec_landed[j], 16 * ITS)
            sp.dma_start(rec_r[:], by_row.rearrange("(r n) w -> r n w", n=2 * P)).then_inc(records_in, 16)
            sp.dma_start(next_r[0:EROWS - 1], by_row[1:1 + (EROWS - 1) * 2 * P, :].rearrange(
                "(r n) w -> r n w", n=2 * P)).then_inc(records_in, 16)
            sp.dma_start(next_r[EROWS - 1:EROWS, 0:2 * P - 1], by_row[1 + (EROWS - 1) * 2 * P:E_PAD, :].rearrange(
                "(o n) w -> o n w", o=1)).then_inc(records_in, 16)
            dense(SDITS - 1, 1)
            sp.wait_ge(cols_f, 1)
            sp.dma_start(row_line.rearrange("(r n) -> r n", n=2 * P), row_r[:]).then_inc(line_out, 16)
            sp.wait_ge(line_out, 16)
            sp.wait_ge(meta_ready, 1)

            def load_rows(pair, half):
                rows = row_line[bass.ds(pair * 2 * P, 2 * P)].rearrange("(o n) -> o n", o=1)
                sp.dma_start(row_b[:, bass.ds(1 + pair * 2 * P, 2 * P)], rows.broadcast_to((P, 2 * P))
                             ).then_inc(row_landed[half], 16)

            load_rows(0, 0)
            load_rows(1, 1)

            def step(it, j, hop, rows_too=True, with_dense=True):
                t = it * UNROLL + j
                if j % 2 == 0:
                    if with_dense:
                        dense(it + SDITS, j // 2)
                    if hop == 1 and rows_too:
                        step_done(sp, row_landed, it, j // 2, by=16)
                        load_rows(it * 2 + j // 2 + 2, j // 2)
                slot = (j - 1) % UNROLL
                step_done(sp, h_row_ready, it, j, 1)
                if hop == 1:
                    sp.dma_start(h1_rows[bass.ds((t - 1) * P, P), :], h_row[:, slot]).then_inc(h_stored[slot], 16)
                    sp.dma_start(side[bass.ds((t - 1) * P, P), 0:C], hT[:, slot].rearrange("p k n -> p (k n)")
                                 ).then_inc(hT_stored[slot], 16)
                else:
                    sp.dma_start(h2_rows[bass.ds((t - 1 - TILES) * P, P), :], h_row[:, slot]
                                 ).then_inc(h_stored[slot], 16)

            def store_p(i, it, j):
                slot = (j - 2) % UNROLL
                step_done(sp, p_ready, it - PH, j, 2)
                sp.dma_start(side[bass.ds(i * P, P), C:C + CO], p_out[:, slot]).then_inc(p_stored[slot], 16)

            def load_h1T(i, it, j):
                slot = (j + 2) % UNROLL
                step_done(sp, p_summed, it - PH, j, 2)
                sp.dma_start(h1T[:, slot], side[bass.ds(i * P, P), 0:P]
                             ).then_inc(side_landed[slot], 16)

            def step2(it, j, load=True):
                t = it * UNROLL + (j - TILES)
                if load:
                    load_h1T(t + 2, it, j)
                step(it, j, 2, with_dense=False)
                store_p(t - 2, it, j)

            for j in range(UNROLL):
                if j:
                    step(0, j, 1)
                else:
                    dense(SDITS, 0)
                    step_done(sp, row_landed, 0, 0, by=16)
                    load_rows(2, 0)

            def hop1_four(it):
                for j in range(UNROLL):
                    step(it, j, 1)

            iterations(sp, 1, PH - 3, hop1_four)
            for it in (PH - 3, PH - 2, PH - 1):
                for j in range(UNROLL):
                    step(it, j, 1, it < PH - 1)
            step(PH, 0, 1, False, with_dense=False)
            for j in range(UNROLL):
                sp.wait_ge(hT_stored[j], 16 * PH)
            for i in range(3):
                load_h1T(i, PH, i - 2)
            for j in range(1, UNROLL):
                load_h1T(j + 2, PH, j)
                step(PH, j, 2, False, with_dense=False)
                if j >= 2:
                    store_p(j - 2, PH, j)

            def hop2_four(it):
                for j in range(UNROLL):
                    step2(it, j)

            iterations(sp, PH + 1, ITS - 1, hop2_four)
            for j in range(UNROLL):
                step2(ITS - 1, j, load=j < 2)
            last = UNROLL - 1
            step_done(sp, h_row_ready, ITS - 1, last)
            sp.dma_start(h2_rows[E_PAD - P:E_PAD, :], h_row[:, last]).then_inc(h_stored[last], 16)
            for j in range(2):
                store_p(TILES - 2 + j, ITS, j)

            for j in range(UNROLL):
                sp.wait_ge(p_stored[j], 16 * PH)

            def load_side(i, slot):
                sp.dma_start(side_in[:, slot], side[bass.ds(i * P, P), P:C + CO]).then_inc(side_landed[slot], 16)

            for i in range(2):
                load_side(i, i)

            def finish(it, j):
                step_done(sp, c_added, (it - ITS) * 2, j, 2)
                load_side(it * UNROLL + (j + 2 - STEPS), (j + 2) % UNROLL)

            for j in range(UNROLL):
                finish(ITS, j)

            def finish_four(it):
                for j in range(UNROLL):
                    finish(it, j)

            iterations(sp, ITS + 1, FITS - 1, finish_four)
            for j in range(UNROLL - 2):
                finish(FITS - 1, j)
            for j in range(UNROLL):
                sp.wait_ge(c_stored[j], 16 * PH)

        @block.gpsimd
        def _(pool):
            nc.gpsimd.memset(ident[:], 0.0)
            nc.gpsimd.memset(ones[:], 1.0).then_inc(consts_set, 1)
            nc.gpsimd.iota(counter_i[:], pattern=[[1, HI]], base=0, channel_multiplier=0).then_inc(counter_set, 1)
            pool.wait_ge(consts_set, 1)
            nc.gpsimd.affine_select(out=ident[:], in_=ident[:], compare_op=ALU.not_equal, fill=1.0,
                                    base=0, pattern=[[-1, P]], channel_multiplier=1).then_inc(consts_set, 1)
            nc.gpsimd.affine_select(out=below[:], in_=ones[:], compare_op=ALU.is_gt, fill=0.0,
                                    base=0, pattern=[[1, P]], channel_multiplier=-1).then_inc(consts_set, 1)
            pool.wait_ge(meta_cleared, 1)
            nc.gpsimd.iota(meta[:, 0:TILES, 2], pattern=[[P, TILES]], base=0,
                           channel_multiplier=1).then_inc(places_set, 1)
            limit_nodes, limit_places = (pool.to_reg(n - 1) for n in (N, E_PAD))

            def go():
                pool.sem_inc(pool_goes, 1)

            def gather(dst_ap, rows, idx, limit, landed):
                nc.gpsimd.indirect_dma_start(
                    dst_ap, None, rows[:, :], bass.IndirectOffsetOnAxis(ap=idx, axis=0),
                    bounds_check=limit, oob_is_err=False).then_inc(landed, 16)

            def scatter(rows, idx, limit, src_ap, landed):
                nc.gpsimd.indirect_dma_start(
                    rows[:, :], bass.IndirectOffsetOnAxis(ap=idx, axis=0), src_ap, None,
                    bounds_check=limit, oob_is_err=False).then_inc(landed, 16)

            def sort(it, j, rows):
                if j % 2 == 0:
                    pool.wait_ge(rec_staged[j // 2], it + 1)
                    go()
                scatter(rows, rec_idx[:, j:j + 1], limit_places, rec_out[:, j], rec_landed[j])

            for first, rows in ((0, by_lo), (PH, by_row)):
                with pool.Fori(first, first + PH) as it:
                    for j in range(UNROLL):
                        sort(it, j, rows)

            pool.wait_ge(table_out, 16)

            def hop1(it, j):
                step_done(pool, h_summed, it, j, UNROLL)
                step_done(pool, staged, it, j)
                go()
                gather(gath[:, j], x, a_idx[:, j, 0:1], limit_nodes, g_landed[j])
                scatter(place_of, a_idx[:, j, 1:2], limit_nodes, a_idx[:, j, 2:3], t_landed[j])

            for j in range(UNROLL):
                hop1(0, j)

            def hop1_four(it):
                for j in range(UNROLL):
                    hop1(it, j)

            iterations(pool, 1, PH, hop1_four)

            for j in range(UNROLL):
                pool.wait_ge(t_landed[j], 16 * PH)

            def ask(j):
                gather(q_got[:, j:j + 1], place_of, q_src[:, j:j + 1], limit_nodes, q_landed[j])

            for j in range(UNROLL):
                pool.wait_ge(q_used[j], 1)
            for j in range(UNROLL):
                ask(j)
            for j in range(UNROLL):
                pool.wait_ge(h_stored[j], 16 * PH)

            def hop2(it, j, more):
                step_done(pool, q_used, it + (1 - PH), j)
                step_done(pool, h_summed, it, j, UNROLL)
                go()
                if more:
                    ask(j)
                gather(gath[:, j], h1_rows, h_idx[:, j:j + 1], limit_places, g_landed[j])

            def hop2_four(it):
                for j in range(UNROLL):
                    hop2(it, j, True)

            iterations(pool, PH, ITS - 1, hop2_four)
            for j in range(UNROLL):
                hop2(ITS - 1, j, False)

            for j in range(UNROLL):
                pool.wait_ge(h_stored[j], 16 * ITS)
            for j in range(2):
                pool.wait_ge(y_stored[j], 16 * ((DENSE - j) // 2 + 1))
            for j in range(UNROLL):
                pool.wait_ge(h_summed[j], ITS)

            def finish(it, j, behind=True, now=True):
                if now:
                    step_done(pool, h_turned, it, j, UNROLL)
                    step_done(pool, h_summed, it, j, UNROLL)
                    step_done(pool, c_staged, it - ITS, j)
                    go()
                    gather(x_dst[:, j], x, c_idx[:, j, 0:1], limit_nodes, c_x_landed[j])
                    gather(gath[:, j], h2_rows, c_idx[:, j, 2:3], limit_places, g_landed[j])
                if behind:
                    step_done(pool, c_ready, it - ITS, j, UNROLL)
                    go()
                    scatter(out, o_idx[:, j:j + 1], limit_nodes, res[:, j], c_stored[j])

            for j in range(UNROLL):
                finish(ITS, j, behind=False)

            def finish_four(it):
                for j in range(UNROLL):
                    finish(it, j)

            iterations(pool, ITS + 1, FITS, finish_four)
            for j in range(UNROLL):
                finish(FITS, j, now=False)

        @block.tensor
        def _(pe):
            pe.wait_ge(setup_done, 2)
            pe.wait_ge(consts_set, 3)

            def turn_x(dit, jd):
                n = dense_nodes(dit * 2 + jd)
                if not n:
                    return
                step_done(pe, x_landed, dit, jd, by=16)
                step_done(pe, xT_ready, dit, jd, 2)
                for r in range(2):
                    for k in range(KC):
                        last = nc.tensor.transpose(ps_x[jd][:, 2 * r + k, 0:n],
                                                   x_in[0:n, jd, r, k * P:(k + 1) * P], ident[0:n, 0:n])
                last.then_inc(x_turned[jd], 1)

            def sum_y(dit, jd):
                n = dense_nodes(dit * 2 + jd)
                if not n:
                    return
                step_done(pe, xT_ready, dit, jd)
                step_done(pe, y_ready, dit, jd, 2)
                for r in range(2):
                    for k in range(KC):
                        last = nc.tensor.matmul(ps_y[jd][0:n, r], xT[:, jd, r, k, 0:n],
                                                w_sb[:, 0, k], start=(k == 0), stop=(k == KC - 1))
                last.then_inc(y_summed[jd], 1)

            def dense(dit):
                for jd in range(2):
                    sum_y(dit, jd)
                    turn_x(dit + 1, jd)

            def wide(bank, width):
                return bank.rearrange("p k n -> p (k n)")[:, 0:width]

            def count(half, times, width, first=False):
                pe.wait_ge(hot_built[half], times)
                for j in range(UNROLL):
                    last = nc.tensor.matmul(wide(ps_h[0], width), ident_b[:], hot[:, half * UNROLL + j, 0:width],
                                            start=first and j == 0, stop=True, skip_group_check=True)
                last.then_inc(hot_used[half], 1)

            for n, width in ((0, LO), (1, HI)):
                if n == 0:
                    turn_x(0, 0)
                    turn_x(0, 1)

                def count_and_dense(g, first=False):
                    dit = g + n * (KITS + PH)
                    if first and n:
                        dense(dit)
                    for half in range(2):
                        count(half, g + n * (KITS + 1 - half) + 1, width, first and half == 0)
                        if not (first and n):
                            sum_y(dit, half)
                            turn_x(dit + 1, half)

                count_and_dense(0, True)
                with pe.Fori(1, KITS) as g:
                    count_and_dense(g)
                count(0, (n + 1) * (KITS + 1), width)
                pe.wait_ge(counts_read, n + 1)
                nc.tensor.matmul(wide(ps_h[1], width), ones[:], counts[:, 0:width], start=True, stop=True)
                nc.tensor.matmul(wide(ps_r[1], width), below[:], counts[:, 0:width],
                                 start=True, stop=True).then_inc(based, 1)
                iterations(pe, n * (KITS + PH) + KITS, (n + 1) * (KITS + PH), dense)

            dense(SDITS - 1)

            pe.wait_ge(cols_f, 2)
            pe.wait_ge(upto_set, 6)
            for half in range(2):
                for n, a in enumerate((col_r, tidx_r, row_r, val_r)):
                    last = nc.tensor.transpose(ps_r[half][:, n, 0:EROWS], a[:, half * P:(half + 1) * P],
                                               ident[0:EROWS, 0:EROWS])
            last.then_inc(meta_turned, 1)
            pe.wait_ge(meta_ready, 1)

            def turn_h(it, j):
                b = (j - 1) % 2
                step_done(pe, hT_ready, it, j, 1)
                step_done(pe, h_row_ready, it, j, 3)
                for k in range(KC):
                    last = nc.tensor.transpose(ps_r[b][:, k], hT[:, (j - 1) % UNROLL, k], ident[:])
                last.then_inc(h_turned[(j - 1) % UNROLL], 1)

            def sum_h(it, j):
                step_done(pe, g_landed, it, j, by=16)
                step_done(pe, s_built, it, j)
                step_done(pe, hT_ready, it, j, 2)
                for k in range(KC):
                    last = nc.tensor.matmul(ps_h[j % 2][:, k], gath[:, j, k * P:(k + 1) * P], S[:, j],
                                            start=True, stop=True)
                last.then_inc(h_summed[j], 1)

            def sum_p(it, j):
                b, slot = (j - 1) % 2, (j - 1) % UNROLL
                step_done(pe, side_landed, it - PH, j, 1, by=16)
                step_done(pe, p_ready, it - PH, j, 3)
                operands = [(h1T[:, slot], w_sb[:, 1, 0])] + [(hT[:, slot, k], w_sb[:, 2, k]) for k in range(KC)]
                for n, (lhsT, w_k) in enumerate(operands):
                    last = nc.tensor.matmul(wide(ps_x[b], CO), lhsT, w_k,
                                            start=(n == 0), stop=(n == len(operands) - 1))
                last.then_inc(p_summed[slot], 1)

            def step(it, j, hop, behind=True, with_dense=True):
                dit, jd = it + SDITS, j // 2
                if with_dense:
                    if j % 2 == 0:
                        sum_y(dit, jd)
                    else:
                        turn_x(dit + 1, jd)
                first_of_hop2 = isinstance(it, int) and it == PH and j == 0
                if first_of_hop2:
                    turn_h(it, j)
                sum_h(it, j)
                if behind and not first_of_hop2:
                    turn_h(it, j)
                if hop == 2 and not first_of_hop2:
                    sum_p(it, j)

            for j in range(UNROLL):
                step(0, j, 1, j > 0)

            def hop1_four(it):
                for j in range(UNROLL):
                    step(it, j, 1)

            iterations(pe, 1, PH - 2, hop1_four)
            for it in (PH - 2, PH - 1):
                for j in range(UNROLL):
                    step(it, j, 1)
            step_done(pe, xT_ready, DITS - 1, 0)
            for j in range(UNROLL):
                step(PH, j, 2, with_dense=False)

            def hop2_four(it):
                for j in range(UNROLL):
                    step(it, j, 2, with_dense=False)

            iterations(pe, PH + 1, ITS, hop2_four)
            turn_h(ITS, 0)
            sum_p(ITS, 0)

            step_done(pe, y_ready, DITS - 1, 0)
            step_done(pe, y_ready, DITS - 2, 1)
            for j in (UNROLL - 2, UNROLL - 1):
                step_done(pe, h_row_ready, ITS - 1, j)
                step_done(pe, p_ready, PH - 1, j)

            def turn_all(it, j):
                step_done(pe, c_x_landed, it - ITS, j, by=16)
                step_done(pe, h_row_ready, it, j, 2)
                for k in range(KC):
                    last = nc.tensor.transpose(ps_x[j % 2][:, k], x_dst[:, j, k * P:(k + 1) * P], ident[:])
                last.then_inc(h_turned[j], 1)

            def sum_all(it, j):
                b, slot = (j - 1) % 2, (j - 1) % UNROLL
                step_done(pe, h_row_ready, it, j, 1)
                step_done(pe, hT_ready, it, j, 1)
                step_done(pe, c_added, (it - ITS) * 2, j, 3)
                step_done(pe, side_landed, it - PH, j, 1, by=16)
                operands = ([(cT[:, slot, k], w_sb[:, 0, k]) for k in range(KC)]
                            + [(side_in[:, slot, 0:P], w_sb[:, 1, 1])]
                            + [(hT[:, slot, k], w_sb[:, 3, k]) for k in range(KC)])
                for n, (lhsT, w_k) in enumerate(operands):
                    last = nc.tensor.matmul(ps_y[b][:, 0], lhsT, w_k,
                                            start=(n == 0), stop=(n == len(operands) - 1))
                last.then_inc(c_y_summed[slot], 1)

            def finish(it, j, behind=True):
                turn_all(it, j)
                sum_h(it, j)
                if behind:
                    sum_all(it, j)

            for j in range(UNROLL):
                finish(ITS, j, j > 0)

            def finish_four(it):
                for j in range(UNROLL):
                    finish(it, j)

            iterations(pe, ITS + 1, FITS, finish_four)
            sum_all(FITS, 0)

        @block.scalar
        def _(act):
            def put_xT(dit, jd):
                n = dense_nodes(dit * 2 + jd)
                if not n:
                    return
                step_done(act, x_turned, dit, jd)
                step_done(act, y_summed, dit, jd, 2)
                nc.scalar.activation(xT[:, jd].rearrange("p r k n -> p (r k) n")[:, :, 0:n],
                                     ps_x[jd][:, :, 0:n], ACT.Copy).then_inc(xT_ready[jd], 1)

            def deviation(dit, jd):
                n = dense_nodes(dit * 2 + jd)
                if n:
                    step_done(act, mv_ready, dit, jd)
                    nc.scalar.activation(std[0:n, jd], mv[0:n, jd, :, 1], ACT.Sqrt, bias=eps[0:n]
                                         ).then_inc(std_ready[jd], 1)

            def norm(dit, jd):
                n = dense_nodes(dit * 2 + jd)
                if not n:
                    return
                step_done(act, nmr_ready, dit, jd)
                step_done(act, y_stored, dit, jd, 2, by=16)
                for r in range(2):
                    last = nc.scalar.activation(y_out[0:n, jd, r], ps_y[jd][0:n, r], ACT.Identity,
                                                bias=nmr[0:n, jd, r:r + 1], scale=rstd[0:n, jd, r:r + 1])
                last.then_inc(y_ready[jd], 1)

            def dense(dit):
                for jd in range(2):
                    put_xT(dit + 1, jd)
                    deviation(dit, jd)
                    norm(dit, jd)

            act.wait_ge(setup_done, 2)
            put_xT(0, 0)
            put_xT(0, 1)
            dense(0)
            iterations(act, 1, SDITS, dense)

            def put_h_row(it, j):
                slot = (j - 1) % UNROLL
                step_done(act, h_turned, it, j, 1)
                step_done(act, h_stored, it, j, 1 + UNROLL, by=16)
                nc.scalar.activation(h_row[:, slot], ps_r[(j - 1) % 2][:, 0:KC].rearrange("p k n -> p (k n)"),
                                     ACT.Copy).then_inc(h_row_ready[slot], 1)

            def put_p(it, j):
                slot = (j - 1) % UNROLL
                step_done(act, p_summed, it - PH, j, 1)
                step_done(act, p_stored, it - PH, j, 1 + UNROLL, by=16)
                nc.scalar.activation(p_out[:, slot], ps_x[(j - 1) % 2][:, 0:KC].rearrange("p k n -> p (k n)"),
                                     ACT.Copy).then_inc(p_ready[slot], 1)

            def step(it, j, behind=True):
                dit, jd = it + SDITS, j // 2
                if j % 2 == 0:
                    if behind:
                        put_h_row(it, j)
                    deviation(dit, jd)
                else:
                    put_xT(dit + 1, jd)
                    put_h_row(it, j)
                    norm(dit, jd)

            for j in range(UNROLL):
                step(0, j, j > 0)

            def hop1_four(it):
                for j in range(UNROLL):
                    step(it, j)

            iterations(act, 1, PH - 2, hop1_four)
            for it in (PH - 2, PH - 1):
                for j in range(UNROLL):
                    step(it, j)
            for j in range(UNROLL):
                put_h_row(PH, j)
                if j:
                    put_p(PH, j)

            def hop2_four(it):
                for j in range(UNROLL):
                    put_h_row(it, j)
                    put_p(it, j)

            iterations(act, PH + 1, ITS, hop2_four)
            put_h_row(ITS, 0)
            put_p(ITS, 0)

            def put_cT(it, j):
                step_done(act, h_turned, it, j)
                step_done(act, c_y_summed, it - ITS, j, UNROLL)
                nc.scalar.activation(cT[:, j], ps_x[j % 2][:, 0:KC], ACT.Copy).then_inc(h_row_ready[j], 1)

            def c_norm(it, j):
                b, slot = (j - 1) % 2, (j - 1) % UNROLL
                step_done(act, c_mv_ready, (it - ITS) * 2, j, 1)
                nc.scalar.activation(std[:, b, 0:1], mv[:, b, 0, 1:2], ACT.Sqrt, bias=eps[:]
                                     ).then_inc(c_std_ready[b], 1)
                step_done(act, c_nmr_ready, (it - ITS) * 2, j, 1)
                step_done(act, c_stored, it - ITS, j, 1 + UNROLL, by=16)
                nc.scalar.activation(res[:, slot], y_sum[:, slot], ACT.Identity, bias=nmr[:, b, 0:1],
                                     scale=rstd[:, b, 0:1]).then_inc(c_ready[slot], 1)

            for jd in range(2):
                act.wait_ge(y_stored[jd], 16 * ((DENSE - jd) // 2 + 1))
            for j in range(UNROLL):
                put_cT(ITS, j)
                if j:
                    c_norm(ITS, j)

            def finish_four(it):
                for j in range(UNROLL):
                    put_cT(it, j)
                    c_norm(it, j)

            iterations(act, ITS + 1, FITS, finish_four)
            c_norm(FITS, 0)

        @block.vector
        def _(dve):
            nc.vector.memset(row_in[:], PAD_ROW)
            nc.vector.memset(col_in[:], 0)
            nc.vector.memset(val_in[:], 0.0)
            nc.vector.memset(nowhere[:], NOWHERE).then_inc(pads_set, 1)
            nc.vector.memset(eps[:], EPS)
            nc.vector.memset(ones_w[:], 1.0)
            nc.vector.memset(row_b[:, 0:1], -2.0)
            nc.vector.memset(digit[:, 0:TILES], -1.0)
            nc.vector.memset(rec[:], 0)
            nc.vector.memset(next_r[:], PAD_ROW)
            nc.vector.memset(meta[:], 0).then_inc(meta_cleared, 1)
            dve.wait_ge(counter_set, 1)
            nc.vector.tensor_copy(counter[:], counter_i[:])
            nc.vector.tensor_copy(counter_h[:], counter_i[:]).then_inc(counter_set, 1)
            dve.wait_ge(edges_in, 6 * 16)
            dve.wait_ge(meta_cleared, 1)
            nc.vector.tensor_copy(rec[:, :, 0], row_in[:])
            nc.vector.tensor_copy(rec[:, :, 1], col_in[:])
            nc.vector.tensor_copy(rec[:, :, 2].bitcast(F32), val_in[:]).then_inc(digits_set, 1)
            dve.wait_ge(consts_set, 2)
            nc.vector.tensor_copy(ident_b[:], ident[:])
            dve.wait_ge(w_in, 16)
            nc.vector.tensor_copy(w_sb[:].rearrange("p h k o -> p k o h"),
                                  w_raw[:].rearrange("p k (o h) -> p k o h", h=HOPS + 1)).then_inc(setup_done, 1)
            dve.wait_ge(setup_done, 1)
            for k in range(KC):
                block_k = w_sb[:, 0, k, k * P:(k + 1) * P]
                last = nc.vector.tensor_tensor(block_k, block_k, ident[:], ALU.add)
            last.then_inc(setup_done, 1)
            dve.wait_ge(counter_set, 2)
            dve.wait_ge(digits_set, 1)

            def digits(n):
                if n == 0:
                    nc.vector.tensor_scalar(digit_i[:], rec[:, :, 0], LO - 1, None, ALU.bitwise_and
                                            ).then_inc(digits_set, 1)
                else:
                    nc.vector.tensor_scalar(digit_i[:], rec[:, :, 0], LO.bit_length() - 1, None,
                                            ALU.logical_shift_right).then_inc(digits_set, 1)
                dve.wait_ge(digits_set, 2 * n + 2)
                nc.vector.tensor_copy(digit[:, TILES:2 * TILES], digit_i[:]).then_inc(digits_set, 1)
                dve.wait_ge(digits_set, 2 * n + 3)

            def rank_of(t, slot):
                nc.vector.tensor_scalar(matched[:, slot], digit[:, bass.ds(t, TILES)],
                                        digit[:, bass.ds(t + TILES, 1)], None, ALU.is_equal, ALU.add,
                                        accum_out=rank[:, bass.ds(t, 1)])

            def one_hot(group, half, width, j):
                made = nc.vector.tensor_scalar(hot[:, half * UNROLL + j, 0:width], counter_h[:, 0:width],
                                               digit[:, bass.ds(group * UNROLL + (j + TILES), 1)], None,
                                               ALU.is_equal)
                if j == UNROLL - 1:
                    made.then_inc(hot_built[half], 1)

            def odd_rank(group, half, j):
                rank_of(group * UNROLL + j, half * UNROLL + j)

            def first_places(n, width):
                dve.wait_ge(hot_used[0], (n + 1) * (KITS + 1))
                dve.wait_ge(hot_used[1], (n + 1) * KITS)
                nc.vector.tensor_copy(counts[:, 0:width], ps_h[0].rearrange("p k n -> p (k n)")[:, 0:width]
                                      ).then_inc(counts_read, 1)
                dve.wait_ge(based, n + 1)
                total = ps_h[1].rearrange("p k n -> p (k n)")[:, 0:width]
                lower = ps_r[1].rearrange("p k n -> p (k n)")[:, 0:width]
                nc.vector.tensor_tensor_scan(upto[:, 0:width], ones_w[:, 0:width], total, 0.0,
                                             ALU.mult, ALU.add).then_inc(upto_set, 1)
                dve.wait_ge(upto_set, 3 * n + 1)
                nc.vector.tensor_tensor(upto[:, 0:width], upto[:, 0:width], total, ALU.subtract).then_inc(upto_set, 1)
                dve.wait_ge(upto_set, 3 * n + 2)
                nc.vector.tensor_tensor(place[:, 0:width], upto[:, 0:width], lower, ALU.add).then_inc(upto_set, 1)
                dve.wait_ge(upto_set, 3 * n + 3)

            def measure(dit, jd):
                n = dense_nodes(dit * 2 + jd)
                if not n:
                    return
                step_done(dve, y_summed, dit, jd)
                for r in range(2):
                    last = nc.vector.bn_stats(stats[0:n, jd, r], ps_y[jd][0:n, r])
                last.then_inc(stats_ready[jd], 1)

            def mean_variance(dit, jd):
                n = dense_nodes(dit * 2 + jd)
                if not n:
                    return
                for r in range(2):
                    last = nc.vector.bn_aggr(mv[0:n, jd, r], stats[0:n, jd, r])
                last.then_inc(mv_ready[jd], 1)

            def stats_done(dit, jd):
                if dense_nodes(dit * 2 + jd):
                    step_done(dve, stats_ready, dit, jd)

            def factors(dit, jd):
                n = dense_nodes(dit * 2 + jd)
                if not n:
                    return
                step_done(dve, std_ready, dit, jd)
                nc.vector.reciprocal(rstd[0:n, jd], std[0:n, jd]).then_inc(rstd_ready[jd], 1)

            def mean_factor(dit, jd):
                n = dense_nodes(dit * 2 + jd)
                if not n:
                    return
                step_done(dve, rstd_ready, dit, jd)
                nc.vector.scalar_tensor_tensor(nmr[0:n, jd], mv[0:n, jd, :, 0], -1.0, rstd[0:n, jd],
                                               ALU.mult, ALU.mult).then_inc(nmr_ready[jd], 1)

            def sort_pair(it, n, half, width, dit):
                t0 = it * UNROLL + (2 * half - n * TILES)
                slots = slice(2 * half, 2 * half + 2)
                measure(dit, half)
                rank_of(t0, 2 * half)
                stats_done(dit, half)
                nc.vector.memset(wait_pad[:], 0.0)
                mean_variance(dit, half)
                for u in range(2):
                    last = nc.vector.scalar_tensor_tensor(
                        picked[:, 2 * half + u, 0:width], counter[:, 0:width], digit[:, bass.ds(t0 + (u + TILES), 1)],
                        place[:, 0:width], ALU.is_equal, ALU.mult,
                        accum_out=place_f[:, 2 * half + u:2 * half + u + 1])
                    if u == 0:
                        factors(dit, half)
                        mean_factor(dit, half)
                last.then_inc(places_picked[half], 1)
                for j in range(2 * half, 2 * half + 2):
                    step_done(dve, rec_landed, it, j, UNROLL, by=16)
                nc.vector.tensor_scalar(rec_out[:, slots].rearrange("p t w -> p (t w)"),
                                        rec[:, bass.ds(t0, 2)].rearrange("p t w -> p (t w)"),
                                        0, None, ALU.bitwise_or)
                dve.wait_ge(places_picked[half], it + 1)
                nc.vector.tensor_tensor(rec_idx[:, slots], place_f[:, slots], rank[:, bass.ds(t0, 2)], ALU.add
                                        ).then_inc(rec_staged[half], 1)

            def dense_alone(dit):
                for half in range(2):
                    measure(dit, half)
                    stats_done(dit, half)
                    nc.vector.memset(wait_pad[:], 0.0)
                    mean_variance(dit, half)
                    factors(dit, half)
                    mean_factor(dit, half)

            def count_eight(g, n, width, more=True):
                dit = g + n * (KITS + PH)
                for half in range(2):
                    group = g * 2 + (2 + half)
                    builds = half == 0 or more
                    measure(dit, half)
                    if builds:
                        dve.wait_ge(hot_used[half], g + n * (KITS + 1 - half) + 1)
                        one_hot(group, half, width, 0)
                    stats_done(dit, half)
                    nc.vector.memset(wait_pad[:], 0.0)
                    mean_variance(dit, half)
                    if builds:
                        odd_rank(group, half, 1)
                        one_hot(group, half, width, 1)
                    factors(dit, half)
                    if builds:
                        one_hot(group, half, width, 2)
                    mean_factor(dit, half)
                    if builds:
                        odd_rank(group, half, 3)
                        one_hot(group, half, width, 3)

            for n, width in ((0, LO), (1, HI)):
                if n:
                    dense_alone(KITS + PH)
                    dve.wait_ge(records_in, 16)
                digits(n)
                if n:
                    dve.wait_ge(hot_used[0], KITS + 1)
                    dve.wait_ge(hot_used[1], KITS)
                for half in range(2):
                    for j in range(UNROLL):
                        if j % 2:
                            odd_rank(half, half, j)
                        one_hot(half, half, width, j)
                if n:
                    for half in range(2):
                        dve.wait_ge(hot_used[half], n * (KITS + 1 - half) + 1)
                        for j in range(UNROLL):
                            if j % 2:
                                odd_rank(2 + half, half, j)
                            one_hot(2 + half, half, width, j)
                with dve.Fori(n, KITS - 1) as g:
                    count_eight(g, n, width)
                count_eight(KITS - 1, n, width, False)
                first_places(n, width)

                def sort_four(it):
                    for half in range(2):
                        sort_pair(it, n, half, width, it + (n + 1) * KITS)

                iterations(dve, n * PH, (n + 1) * PH, sort_four)

            dense_alone(SDITS - 1)
            nc.vector.memset(hT[:], 0.0)
            nc.vector.memset(x_dst[:], 0.0).then_inc(meta_cleared, 1)
            dve.wait_ge(records_in, 4 * 16)
            nc.vector.tensor_copy(row_r[:], rec_r[:, :, 0]).then_inc(cols_f, 1)
            nc.vector.tensor_copy(col_r[:], rec_r[:, :, 1])
            nc.vector.tensor_copy(val_r[:], rec_r[:, :, 2].bitcast(F32))
            nc.vector.tensor_tensor(last_r[:], rec_r[:, :, 0], next_r[:, :, 0], ALU.not_equal).then_inc(shifted, 1)
            dve.wait_ge(shifted, 1)
            nc.vector.scalar_tensor_tensor(tidx_r[:], row_r[:], float(-NOWHERE), last_r[:],
                                           ALU.add, ALU.mult).then_inc(shifted, 1)
            dve.wait_ge(shifted, 2)
            nc.vector.tensor_scalar(tidx_r[:], tidx_r[:], float(NOWHERE), None, ALU.add).then_inc(cols_f, 1)
            dve.wait_ge(meta_turned, 1)
            dve.wait_ge(places_set, 1)
            dve.wait_ge(meta_cleared, 2)
            for half in range(2):
                tiles = slice(half, TILES, 2)
                nc.vector.tensor_copy(meta[:, tiles, 0], ps_r[half][:, 0, 0:EROWS])
                nc.vector.tensor_copy(meta[:, tiles, 1], ps_r[half][:, 1, 0:EROWS])
                nc.vector.tensor_copy(r_col[:, tiles], ps_r[half][:, 2, 0:EROWS])
                last = nc.vector.tensor_copy(v_col[:, tiles], ps_r[half][:, 3, 0:EROWS])
            last.then_inc(meta_ready, 1)
            dve.wait_ge(meta_ready, 1)

            def stage(it, j):
                step_done(dve, g_landed, it, j, UNROLL, by=16)
                step_done(dve, t_landed, it, j, UNROLL, by=16)
                nc.vector.tensor_copy(a_idx[:, j], meta[:, bass.ds(it * UNROLL + j, 1), 0:3].rearrange(
                    "p o n -> p (o n)")).then_inc(staged[j], 1)

            def ask_later(i, j):
                nc.vector.tensor_copy(q_src[:, j:j + 1], meta[:, bass.ds(i, 1), 0]).then_inc(q_used[j], 1)

            def use_place(it, j):
                i = it * UNROLL + (j - TILES)
                step_done(dve, q_landed, it - PH, j, by=16)
                nc.vector.scalar_tensor_tensor(v_col[:, bass.ds(i + TILES, 1)], q_got[:, j:j + 1], float(E_PAD),
                                               v_col[:, bass.ds(i, 1)], ALU.is_lt, ALU.mult)
                nc.vector.tensor_copy(h_idx[:, j:j + 1], q_got[:, j:j + 1])
                nc.vector.tensor_copy(meta[:, bass.ds(i, 1), 3], q_got[:, j:j + 1])
                ask_later(i + UNROLL, j)

            def build(it, j, hop):
                i = it * UNROLL + (j - (hop - 1) * TILES)
                if hop == 1:
                    step_done(dve, row_landed, it, j // 2, by=16)
                if hop == 2:
                    step_done(dve, q_used, it - PH + 1, j)
                nc.vector.tensor_scalar(S[:, j], row_b[:, bass.ds(i * P + 1, P)], r_col[:, bass.ds(i, 1)],
                                        v_col[:, bass.ds(i + (TILES if hop > 1 else 0), 1)],
                                        ALU.is_equal, ALU.mult)
                nc.vector.tensor_scalar(same[:, j], row_b[:, bass.ds(i * P + 1, P)], row_b[:, bass.ds(i * P, 1)],
                                        None, ALU.is_equal).then_inc(s_built[j], 1)

            def carry(it, j):
                step_done(dve, h_summed, it, j)
                step_done(dve, s_built, it, j)
                step_done(dve, hT_ready, it, j, 1)
                for k in range(KC):
                    last = nc.vector.scalar_tensor_tensor(
                        hT[:, j, k], same[:, j], hT[:, (j - 1) % UNROLL, k, P - 1:P], ps_h[j % 2][:, k],
                        ALU.mult, ALU.add)
                last.then_inc(hT_ready[j], 1)

            def next_of(it, j, ahead):
                return it + (j + ahead) // UNROLL, (j + ahead) % UNROLL

            def step(it, j, hop, stages=True, builds=True, with_dense=True):
                dit, jd = it + SDITS, j // 2
                if hop == 1 or isinstance(it, int) and it == PH:
                    step_done(dve, h_turned, it, j, UNROLL)
                    step_done(dve, hT_stored, it, j, UNROLL, by=16)
                else:
                    step_done(dve, p_summed, it - PH, j, UNROLL)
                carry(it, j)
                if with_dense and j % 2 == 0:
                    measure(dit, jd)
                if hop == 1:
                    stage(*next_of(it, j, 3))
                elif stages:
                    use_place(*next_of(it, j, 3))
                if with_dense and j % 2 == 1:
                    factors(dit, jd)
                if builds:
                    build(*next_of(it, j, 2), hop)
                if with_dense:
                    if j % 2 == 0:
                        stats_done(dit, jd)
                        nc.vector.memset(wait_pad[:], 0.0)
                        mean_variance(dit, jd)
                    else:
                        mean_factor(dit, jd)

            for j in range(UNROLL - 1):
                stage(0, j)
            for j in range(2):
                build(0, j, 1)
            for j in range(UNROLL):
                step(0, j, 1)

            def hop1_four(it):
                for j in range(UNROLL):
                    step(it, j, 1)

            iterations(dve, 1, PH - 1, hop1_four)
            for j in range(UNROLL):
                step(PH - 1, j, 1, builds=j < UNROLL - 2)
            for j in range(UNROLL):
                ask_later(j, j)
            for j in range(UNROLL - 1):
                use_place(PH, j)
            for j in range(2):
                build(PH, j, 2)
            for j in range(UNROLL):
                step(PH, j, 2, with_dense=False)

            def hop2_four(it):
                for j in range(UNROLL):
                    step(it, j, 2, with_dense=False)

            iterations(dve, PH + 1, ITS - 1, hop2_four)
            for j in range(UNROLL):
                step(ITS - 1, j, 2, j == 0, j < UNROLL - 2, with_dense=False)

            def c_stage(it, j):
                step_done(dve, c_x_landed, it - ITS, j, UNROLL, by=16)
                step_done(dve, g_landed, it, j, UNROLL, by=16)
                nc.vector.tensor_copy(c_idx[:, j], meta[:, bass.ds(it * UNROLL + (j - STEPS), 1), 1:4].rearrange(
                    "p o n -> p (o n)")).then_inc(c_staged[j], 1)

            def c_add(it, j):
                b, slot = (j - 1) % 2, (j - 1) % UNROLL
                step_done(dve, c_y_summed, it - ITS, j, 1)
                step_done(dve, side_landed, it - PH, j, 1, by=16)
                step_done(dve, c_ready, it - ITS, j, 1 + UNROLL)
                nc.vector.tensor_tensor(y_sum[:, slot], ps_y[b][:, 0], side_in[:, slot, P:P + CO], ALU.add
                                        ).then_inc(c_added[b], 1)

            def c_measure(it, j):
                b, slot = (j - 1) % 2, (j - 1) % UNROLL
                step_done(dve, c_added, (it - ITS) * 2, j, 1)
                nc.vector.bn_stats(stats[:, b, 0], y_sum[:, slot]).then_inc(c_stats_ready[b], 1)
                step_done(dve, c_stored, it - ITS, j, 1 + UNROLL, by=16)
                step_done(dve, c_stats_ready, (it - ITS) * 2, j, 1)
                nc.vector.memset(wait_pad[:], 0.0)
                nc.vector.tensor_copy(o_idx[:, slot:slot + 1], meta[:, bass.ds(it * UNROLL + (j - 1 - STEPS), 1), 1])
                nc.vector.bn_aggr(mv[:, b, 0], stats[:, b, 0]).then_inc(c_mv_ready[b], 1)

            def c_factors(it, j):
                b = (j - 1) % 2
                step_done(dve, c_std_ready, (it - ITS) * 2, j, 1)
                nc.vector.reciprocal(rstd[:, b, 0:1], std[:, b, 0:1]).then_inc(c_rstd_ready[b], 1)
                step_done(dve, c_rstd_ready, (it - ITS) * 2, j, 1)
                nc.vector.scalar_tensor_tensor(nmr[:, b, 0:1], mv[:, b, 0, 0:1], -1.0, rstd[:, b, 0:1],
                                               ALU.mult, ALU.mult).then_inc(c_nmr_ready[b], 1)

            def finish(it, j, behind=True, builds=True):
                step_done(dve, c_y_summed, it - ITS, j, UNROLL)
                carry(it, j)
                if behind:
                    c_add(it, j)
                c_stage(*next_of(it, j, 3))
                if behind:
                    c_measure(it, j)
                if builds:
                    build(*next_of(it, j, 2), 3)
                if behind:
                    c_factors(it, j)

            for j in range(UNROLL):
                dve.wait_ge(q_used[j], PH + 1)
                dve.wait_ge(p_summed[j], PH)
            for j in range(UNROLL - 1):
                c_stage(ITS, j)
            for j in range(2):
                build(ITS, j, 3)
            for j in range(UNROLL):
                finish(ITS, j, j > 0)

            def finish_four(it):
                for j in range(UNROLL):
                    finish(it, j)

            iterations(dve, ITS + 1, FITS - 1, finish_four)
            for j in range(UNROLL):
                finish(FITS - 1, j, builds=j < UNROLL - 2)
            c_add(FITS, 0)
            c_measure(FITS, 0)
            c_factors(FITS, 0)


_INS = ['x', 'src', 'dst', 'edge_weight', 'L0_gnn_weight']


def kernel(**inputs):
    import numpy as _np
    import concourse.bacc as _bacc
    from concourse import mybir as _mybir
    from concourse.bass_utils import run_bass_kernel_spmd as _run

    nc = _bacc.Bacc("TRN2", target_bir_lowering=False, num_devices=1)
    arrays, args = {}, []
    for name in _INS:
        a = _np.ascontiguousarray(inputs[name])
        arrays[f"in_{name}_dram"] = a
        args.append(nc.dram_tensor(f"in_{name}_dram", a.shape, _mybir.dt.from_np(a.dtype), kind="ExternalInput").ap())
    shape = inputs['x'].shape
    args.append(nc.dram_tensor("out_0_dram", shape, _mybir.dt.float32, kind="ExternalOutput").ap())
    gnn_program(nc, *args)
    r = _run(nc, [arrays], core_ids=[0])
    return r.results[0]["out_0_dram"]
```
